# Optimizing a Trainium2 kernel written in Bass

```python
import numpy as np
import jax
import jax.numpy as jnp

def _softmax(x, axis=-1):
    return jax.nn.softmax(x, axis=axis)

def _gelu(x):
    return jax.nn.gelu(x, approximate=True)

def _silu(x):
    return jax.nn.silu(x)

def _sigmoid(x):
    return jax.nn.sigmoid(x)

def _layernorm(x, axis=-1, eps=1e-05):
    m = jnp.mean(x, axis=axis, keepdims=True)
    v = jnp.var(x, axis=axis, keepdims=True)
    return (x - m) / jnp.sqrt(v + eps)

def _scatter_add(tgt, idx, src, axis=0):
    return tgt.at[idx].add(src)

def _segment_sum(src, seg, n):
    return jax.ops.segment_sum(src, seg, n)
kernel_name = 'mk_seq_postln_d1_jaxref_r8_d3b959'

def setup_inputs(seed: int=0):
    np.random.seed(seed)
    _w = jnp.asarray

    def _L0_attn_setup():
        import jax, jax.numpy as jnp
        import numpy as np
        D_MODEL, N_HEADS, N_KV, HEAD_DIM, D_LAT = (128, 8, 2, 128, 32)
        N_REP = N_HEADS // N_KV
        B, T = (2, 256)
        key = jax.random.key(seed)
        ks = jax.random.split(key, 8)
        s = lambda fan_in: 1.0 / np.sqrt(fan_in)
        return {'x': jax.random.normal(ks[0], (B, T, D_MODEL), jnp.float32), 'wq': jax.random.normal(ks[1], (D_MODEL, N_HEADS * HEAD_DIM), jnp.float32) * s(D_MODEL), 'wk_down': jax.random.normal(ks[2], (D_MODEL, N_KV * D_LAT), jnp.float32) * s(D_MODEL), 'wv_down': jax.random.normal(ks[3], (D_MODEL, N_KV * D_LAT), jnp.float32) * s(D_MODEL), 'wk_up': jax.random.normal(ks[4], (D_LAT, HEAD_DIM), jnp.float32) * s(D_LAT), 'wv_up': jax.random.normal(ks[5], (D_LAT, HEAD_DIM), jnp.float32) * s(D_LAT), 'wo': jax.random.normal(ks[6], (N_HEADS * HEAD_DIM, D_MODEL), jnp.float32) * s(N_HEADS * HEAD_DIM)}
    _L0_attn_in = _L0_attn_setup()

    def _L0_ffn_setup():
        import jax, jax.numpy as jnp
        import numpy as np
        D_IN, D_HID = (128, 512)

        def _ternary(key, shape):
            return jax.random.randint(key, shape, -1, 2).astype(jnp.float32)

        def _tlin(x, w, s):
            return jnp.einsum('bsi,oi->bso', x, w) * s
        key = jax.random.key(seed)
        ks = jax.random.split(key, 12)
        inv = lambda fan: 1.0 / np.sqrt(fan).astype(np.float32)
        return {'x': jax.random.normal(ks[0], (4, 256, D_IN), dtype=jnp.float32), 'w1_w': _ternary(ks[1], (D_HID, D_IN)), 'w1_s': jax.random.uniform(ks[2], (D_HID,), dtype=jnp.float32) * inv(D_IN), 'w2_w': _ternary(ks[3], (D_HID, D_IN)), 'w2_s': jax.random.uniform(ks[4], (D_HID,), dtype=jnp.float32) * inv(D_IN), 'h1_w': _ternary(ks[5], (D_HID, D_HID)), 'h1_s': jax.random.uniform(ks[6], (D_HID,), dtype=jnp.float32) * inv(D_HID), 'h2_w': _ternary(ks[7], (D_HID, D_HID)), 'h2_s': jax.random.uniform(ks[8], (D_HID,), dtype=jnp.float32) * inv(D_HID), 'w3_w': _ternary(ks[9], (D_IN, D_HID)), 'w3_s': jax.random.uniform(ks[10], (D_IN,), dtype=jnp.float32) * inv(D_HID)}
    _L0_ffn_in = _L0_ffn_setup()
    _d = {'L0_attn_x': _L0_attn_in['x'], 'L0_attn_wq': _L0_attn_in['wq'], 'L0_attn_wk_down': _L0_attn_in['wk_down'], 'L0_attn_wv_down': _L0_attn_in['wv_down'], 'L0_attn_wk_up': _L0_attn_in['wk_up'], 'L0_attn_wv_up': _L0_attn_in['wv_up'], 'L0_attn_wo': _L0_attn_in['wo'], 'L0_ffn_w1_w': _L0_ffn_in['w1_w'], 'L0_ffn_w1_s': _L0_ffn_in['w1_s'], 'L0_ffn_w2_w': _L0_ffn_in['w2_w'], 'L0_ffn_w2_s': _L0_ffn_in['w2_s'], 'L0_ffn_h1_w': _L0_ffn_in['h1_w'], 'L0_ffn_h1_s': _L0_ffn_in['h1_s'], 'L0_ffn_h2_w': _L0_ffn_in['h2_w'], 'L0_ffn_h2_s': _L0_ffn_in['h2_s'], 'L0_ffn_w3_w': _L0_ffn_in['w3_w'], 'L0_ffn_w3_s': _L0_ffn_in['w3_s']}
    _x0 = _d['L0_attn_x']
    _d['L0_attn_x'] = jax.random.normal(jax.random.fold_in(jax.random.key(seed), 1), (16, 512, 128), dtype=_x0.dtype)
    del _x0
    return _d

def reference(L0_attn_x, L0_attn_wq, L0_attn_wk_down, L0_attn_wv_down, L0_attn_wk_up, L0_attn_wv_up, L0_attn_wo, L0_ffn_w1_w, L0_ffn_w1_s, L0_ffn_w2_w, L0_ffn_w2_s, L0_ffn_h1_w, L0_ffn_h1_s, L0_ffn_h2_w, L0_ffn_h2_s, L0_ffn_w3_w, L0_ffn_w3_s):

    def _L0_attn_ref(x, wq, wk_down, wv_down, wk_up, wv_up, wo):
        import jax, jax.numpy as jnp
        import numpy as np
        D_MODEL, N_HEADS, N_KV, HEAD_DIM, D_LAT = (128, 8, 2, 128, 32)
        N_REP = N_HEADS // N_KV
        B, T = (2, 256)
        Bq, Tq, _ = x.shape
        scale = HEAD_DIM ** (-0.5)
        q = (x @ wq).reshape(Bq, Tq, N_KV, N_REP, HEAD_DIM)
        k_lat = (x @ wk_down).reshape(Bq, Tq, N_KV, D_LAT)
        v_lat = (x @ wv_down).reshape(Bq, Tq, N_KV, D_LAT)
        k = jnp.einsum('bkhl,ld->bkhd', k_lat, wk_up)
        v = jnp.einsum('bkhl,ld->bkhd', v_lat, wv_up)
        scores = jnp.einsum('bqhrd,bkhd->bhrqk', q, k) * scale
        causal = jnp.tril(jnp.ones((Tq, Tq), dtype=bool))
        scores = jnp.where(causal, scores, jnp.finfo(scores.dtype).min)
        probs = jax.nn.softmax(scores, axis=-1)
        y = jnp.einsum('bhrqk,bkhd->bqhrd', probs, v)
        y = y.reshape(Bq, Tq, N_HEADS * HEAD_DIM)
        return y @ wo

    def _L0_ffn_ref(x, w1_w, w1_s, w2_w, w2_s, h1_w, h1_s, h2_w, h2_s, w3_w, w3_s):
        import jax, jax.numpy as jnp
        import numpy as np
        D_IN, D_HID = (128, 512)

        def _ternary(key, shape):
            return jax.random.randint(key, shape, -1, 2).astype(jnp.float32)

        def _tlin(x, w, s):
            return jnp.einsum('bsi,oi->bso', x, w) * s
        h = jax.nn.silu(_tlin(x, w1_w, w1_s)) * _tlin(x, w2_w, w2_s)
        h = jax.nn.gelu(_tlin(h, h1_w, h1_s), approximate=False)
        h = jax.nn.gelu(_tlin(h, h2_w, h2_s), approximate=False)
        return _tlin(h, w3_w, w3_s)
    x = L0_attn_x
    x = _layernorm(x + _L0_attn_ref(x, L0_attn_wq, L0_attn_wk_down, L0_attn_wv_down, L0_attn_wk_up, L0_attn_wv_up, L0_attn_wo), axis=-1)
    x = _layernorm(x + _L0_ffn_ref(x, L0_ffn_w1_w, L0_ffn_w1_s, L0_ffn_w2_w, L0_ffn_w2_s, L0_ffn_h1_w, L0_ffn_h1_s, L0_ffn_h2_w, L0_ffn_h2_s, L0_ffn_w3_w, L0_ffn_w3_s), axis=-1)
    return x

_drawn_inputs = setup_inputs


def setup_inputs(seed=0):
    import zlib

    import numpy as np

    out = dict(_drawn_inputs(seed))
    spreads = {}
    factors = {'L0_ffn_w1_w': 8.0,
     'L0_ffn_w1_s': 8.0,
     'L0_ffn_w2_w': 8.0,
     'L0_ffn_w2_s': 8.0,
     'L0_ffn_h1_w': 8.0,
     'L0_ffn_h1_s': 8.0,
     'L0_ffn_h2_w': 8.0,
     'L0_ffn_h2_s': 8.0,
     'L0_ffn_w3_w': 8.0,
     'L0_ffn_w3_s': 8.0}
    for name, (base, spread) in spreads.items():
        noise = np.random.default_rng([zlib.crc32(name.encode()), seed]).standard_normal(out[name].shape)
        drawn = base * np.exp(spread * noise) if base else spread * noise
        out[name] = jnp.asarray(drawn.astype(out[name].dtype))
    for name, factor in factors.items():
        out[name] = (out[name] * factor).astype(out[name].dtype)
    return out
```

```python
from contextlib import ExitStack

import concourse.bass as bass
from concourse import mybir

F32 = mybir.dt.float32
F32R = mybir.dt.float32r
I32 = mybir.dt.int32
ALU = mybir.AluOpType
ACT = mybir.ActivationFunctionType
AX_X = mybir.AxisListType.X

P = 128
LOWEST = -3.0e38
EPS = 1e-5
RSQRT_MAGIC = 0x5F3759DF
NEWTON = 3


class Count:

    def __init__(self, reg, mul=1, add=0):
        self.reg, self.mul, self.add = reg, mul, add

    def __add__(self, n):
        return Count(self.reg, self.mul, self.add + n)

    def __sub__(self, n):
        return self + -n

    def __mul__(self, n):
        return Count(self.reg, self.mul * n, self.add * n)

    __radd__, __rmul__ = __add__, __mul__

    def value(self):
        return (self.reg * self.mul if self.mul != 1 else self.reg) + self.add if self.add else self.reg * self.mul


def value(n):
    return n.value() if isinstance(n, Count) else n


def build_layer(nc, xT, wqT, wk_down, wv_down, wk_upT, wv_upT, wo, w1T, w1_s, w2T, w2_s, h1T, h1_s, h2T, h2_s, w3T,
                w3_s, out):
    NB, D, T = xT.shape
    HD, H, _ = wqT.shape
    L = wk_upT.shape[1]
    G = wk_down.shape[1] // L
    R = H // G
    F = w1T.shape[1]
    FC = F // P
    NI = T // P
    K3 = 3 * L
    K3M = K3 + 2
    SCALE = float(HD) ** -0.5
    PREP_MQ = 1 + 2 * 3 * G + 2
    PREP_WVO = PREP_MQ + H + 2 + G + 1
    PREP_RAW = PREP_WVO + 4 + 2 * FC + 2 + 2
    PREP_ALL = PREP_RAW + 4 + 2
    NM_STEPS = 2 + P // 32
    NEWTON_STEPS = 4 * NEWTON
    assert D == P and HD == P and FC == 2 * G and T == 512 and R * L == P and 2 * R * NI == 32 and G == 2 and NB % 2 == 0

    items = [(g, i, j) for g in range(G) for i in range(NI) for j in range(i + 1)]
    NK = len(items)
    units = [(g, i) for g in range(G) for i in range(NI)]
    NU = len(units)
    last_of_unit = {items.index((g, i, i)): u for u, (g, i) in enumerate(units)}
    max_units = [[(g, i, h) for h in range(h0, h0 + (2 if i < 2 else 1))]
                 for g in range(G) for i in range(NI) for h0 in range(0, R, 2 if i < 2 else 1)]
    NX = len(max_units)
    XG = NX // G
    NKG = NK // G
    max_at = [2, 1, 1, 1, 2, 1, 1, 1, 1, 1]
    NM_AT = 4
    OUT_AT, VAR_AT, Q_AT, X_AT = 2, 4, 5, 8
    XL = sum(max_at[NM_AT + 1:])
    assert len(max_at) == NKG and sum(max_at) == XG

    with ExitStack() as ctx:
        def sb(name, shape, dt=F32):
            return ctx.enter_context(nc.sbuf_tensor(name, shape, dt))

        def pb(name, shape=(P, 512)):
            return ctx.enter_context(nc.psum_tensor(name, list(shape), F32))

        def sem(name):
            return ctx.enter_context(nc.semaphore(name))

        mq_f = sb("mq_f", [P, H * L])
        mq_hi = sb("mq_hi", [P, H * L], F32R)
        mq_lo = sb("mq_lo", [P, H * L], F32R)
        wk_f = sb("wk_f", [P, G * L])
        wk_hi = sb("wk_hi", [P, G, 3, L], F32R)
        wk_lo = sb("wk_lo", [P, G, 3, L], F32R)
        wv_f = sb("wv_f", [P, G * L])
        wku_f = sb("wku_f", [P, L])
        wvu_f = sb("wvu_f", [P, R, L])
        wvo = sb("wvo", [P, G, P])
        wvo_mean = sb("wvo_mean", [P, G])
        w1_hi, w1_lo = sb("w1_hi", [P, F], F32R), sb("w1_lo", [P, F], F32R)
        w2_hi, w2_lo = sb("w2_hi", [P, F], F32R), sb("w2_lo", [P, F], F32R)
        h1_hi, h1_lo = sb("h1_hi", [P, FC, F], F32R), sb("h1_lo", [P, FC, F], F32R)
        h2_hi, h2_lo = sb("h2_hi", [P, FC, F], F32R), sb("h2_lo", [P, FC, F], F32R)
        w3_hi, w3_lo = sb("w3_hi", [P, FC, P], F32R), sb("w3_lo", [P, FC, P], F32R)
        w3_mean = sb("w3_mean", [P, FC])
        s1h = sb("s1h", [P, FC])
        s12h = sb("s12h", [P, FC])
        s2 = sb("s2", [P, FC])
        sh1 = sb("sh1", [P, FC])
        sh2 = sb("sh2", [P, FC])
        s3_row = sb("s3_row", [P, P])
        center_f = sb("center_f", [P, P])
        center = sb("center", [P, P], F32R)
        mean_of = sb("mean_of", [P, P])
        max_mask = sb("max_mask", [P, T])
        x_f = sb("x_f", [P, 2, T])
        x_hi = sb("x_hi", [P, 2, T], F32R)
        x_lo = sb("x_lo", [P, 2, T], F32R)
        q_hi = sb("q_hi", [P, G, T], F32R)
        q_lo = sb("q_lo", [P, G, T], F32R)
        qs = sb("qs", [P, 2, H * T], F32R)
        ks = sb("ks", [P, 2, G, T], F32R)
        vs = sb("vs", [P, 2, NI, G, 2 * L])
        probs = sb("probs", [P, 4, T])
        rden = sb("rden", [L, 2, T])
        ys = sb("ys", [P, 2, G, T])
        mx = sb("mx", [P, H * NI])
        nm = sb("nm", [P, 2, R * NI], F32R)
        nmT = sb("nmT", [2 * R * NI, P], F32R)
        rc = sb("rc", [P, T])
        sq = sb("sq", [P, T])
        rstd = sb("rstd", [P, T])
        x1 = sb("x1", [P, NB * T])
        eps_col = sb("eps_col", [P, 1])
        gate = sb("gate", [P, NX + NU])
        tmp = sb("tmp", [P, 8, T])
        c_act = sb("c_act", [P, FC * T], F32R)
        a_hi = [qs[:, 0, c * T:(c + 1) * T] for c in range(FC)]
        a_lo = [qs[:, 0, (FC + c) * T:(FC + c + 1) * T] for c in range(FC)]
        b_hi = [qs[:, 1, c * T:(c + 1) * T] for c in range(FC)]
        b_lo = [qs[:, 1, (FC + c) * T:(FC + c + 1) * T] for c in range(FC)]
        c_hi = [(q_hi, q_lo)[c // G][:, c % G, :] for c in range(FC)]
        c_lo = [c_act[:, c * T:(c + 1) * T] for c in range(FC)]
        raw_lo = tmp[:, 0:4, :].rearrange("p a n -> p (a n)")
        raw_hi = tmp[:, 4:8, :].rearrange("p a n -> p (a n)")
        wq_raw = raw_lo[:, 0:H * P].rearrange("p (h d) -> p h d", h=H)
        wo_raw = raw_lo[:, H * P:2 * H * P].rearrange("p (h d) -> p h d", h=H)
        t_act = [tmp[:, n, :] for n in range(2)]
        u_act = [tmp[:, 2 + n, :] for n in range(2)]
        g_act = [tmp[:, 4 + n, :] for n in range(2)]
        y_out = [tmp[:, 6 + n, :] for n in range(2)]
        var_eps, var_half = rc, ys[:, 0, 0, :]
        newton_t, three_halves = rstd, ys[:, 0, 1, :]
        newton_y = sb("newton_y", [P, T])

        bank_a, bank_b = pb("bank_a"), pb("bank_b")
        bank_max = [pb("bank_max0"), pb("bank_max1")]
        bank_s = [pb("bank_s0"), pb("bank_s1")]
        bank_pv = [pb("bank_pv0"), pb("bank_pv1")]

        s_load = {n: sem(f"s_load_{n}") for n in ("attn", "small", "w123", "h1", "h2")}
        s_x = sem("s_x")
        s_x_again = sem("s_x_again")
        s_const = sem("s_const")
        s_prep_pe = sem("s_prep_pe")
        s_prep = sem("s_prep")
        s_x_hi, s_x_lo = sem("s_x_hi"), sem("s_x_lo")
        s_v, s_q, s_k = sem("s_v"), sem("s_q"), sem("s_k")
        s_v_out = sem("s_v_out")
        s_q_hi, s_q_lo = sem("s_q_hi"), sem("s_q_lo")
        s_k_hi, s_k_lo = sem("s_k_hi"), sem("s_k_lo")
        s_qdma = [sem(f"s_qdma{g}") for g in range(G)]
        s_sx = sem("s_sx")
        s_mx = sem("s_mx")
        s_nm = sem("s_nm")
        s_mdma = [sem(f"s_mdma{g}") for g in range(G)]
        s_st = sem("s_st")
        s_exp = sem("s_exp")
        s_diag = sem("s_diag")
        s_pv = sem("s_pv")
        s_ln, s_rden = sem("s_ln"), sem("s_rden")
        s_y = sem("s_y")
        s_o, s_rc, s_sq, s_var = sem("s_o"), sem("s_rc"), sem("s_sq"), sem("s_var")
        s_lnv, s_rstd, s_x1 = sem("s_lnv"), sem("s_rstd"), sem("s_x1")
        f_x_hi, f_x_lo = sem("f_x_hi"), sem("f_x_lo")
        f_a, f_b, f_c, f_d = sem("f_a"), sem("f_b"), sem("f_c"), sem("f_d")
        f_t = sem("f_t")
        f_u, f_z, f_ah, f_al = sem("f_u"), sem("f_z"), sem("f_ah"), sem("f_al")
        f_bg, f_bl, f_cg, f_cl = sem("f_bg"), sem("f_bl"), sem("f_cg"), sem("f_cl")
        f_sq, f_var, f_v, f_g, f_n, f_y, f_store = sem("f_sq"), sem("f_var"), sem("f_v"), sem("f_g"), sem("f_n"), sem("f_y"), [sem("f_store0"), sem("f_store1")]

        def wait(eng, s, n):
            if not isinstance(n, int) or n > 0:
                eng.wait_ge(s, value(n))

        def batches(eng, body):
            body(0, 0, False, 2)
            body(1, 1, True, 2)
            with eng.Fori(2, NB - 3, 2) as reg:
                b = Count(reg)
                body(b, 0, True, 2)
                body(b + 1, 1, True, 2)
            body(NB - 2, 0, True, 1)
            body(NB - 1, 1, True, 0)

        def steps(before, left):
            seq = []
            if left:
                seq.append(("v", 1))
            nx = XG + XL
            for k in range(NK):
                ended = last_of_unit.get((k - 1) % NK)
                if ended is not None and k == 0:
                    ended = -1 if before else None
                seq.append(("pv", k))
                if ended is not None:
                    seq.append(("den", ended))
                if k + 2 < NK or left:
                    seq.append(("st", k + 2))
                if k == OUT_AT and before:
                    seq.append(("o", -1))
                if k == VAR_AT and before:
                    seq.append(("var", -1))
                if k == Q_AT and left:
                    seq.append(("q", 1 * G + 1))
                if k == Q_AT + 1 and left:
                    seq.append(("k", 1 * G + 1))
                if k == X_AT and left == 2:
                    seq.append(("x", 2))
                if k == NKG + Q_AT and left == 2:
                    seq.append(("q", 2 * G))
                if k == NKG + Q_AT + 1 and left == 2:
                    seq.append(("k", 2 * G))
                for _ in range(max_at[k % NKG]):
                    if nx < NX or left:
                        seq.append(("mx", nx))
                        nx += 1
                if ended is not None:
                    seq.append(("y", ended))
                if k % NKG == NM_AT and (k < NKG or left):
                    seq.append(("nm", k // NKG + 1))
            return seq

        def mlp_order(left):
            a = [("a", c) for c in range(FC)] if left else []
            c = [("c", c) for c in range(FC)]
            return a[0:2] + c[0:1] + a[2:3] + c[1:2] + a[3:4] + c[2:]

        block = ctx.enter_context(nc.Block())

        @block.sync
        def _(sp):
            sp.dma_start(x_f[:, 0, :], xT[0]).then_inc(s_x, 16)
            sp.dma_start(wq_raw, wqT).then_inc(s_load["attn"], 16)
            sp.dma_start(wku_f[:], wk_upT).then_inc(s_load["attn"], 16)
            sp.dma_start(wk_f[:], wk_down).then_inc(s_load["attn"], 16)
            sp.dma_start(wv_f[:], wv_down).then_inc(s_load["attn"], 16)
            sp.dma_start(wo_raw, wo).then_inc(s_load["attn"], 16)
            for r in range(R):
                sp.dma_start(wvu_f[:, r, :], wv_upT).then_inc(s_load["attn"], 16)
            sp.dma_start(raw_hi[:, 0:F], w1T).then_inc(s_load["w123"], 16)
            sp.dma_start(raw_hi[:, F:2 * F], w2T).then_inc(s_load["w123"], 16)
            sp.dma_start(raw_hi[:, 2 * F:3 * F].rearrange("p (c n) -> p c n", c=FC), w3T).then_inc(s_load["w123"], 16)
            for dst, src in ((s1h, w1_s), (s2, w2_s), (sh1, h1_s), (sh2, h2_s)):
                sp.dma_start(dst[:], src).then_inc(s_load["small"], 16)
            sp.dma_start(s3_row[:], w3_s.partition_broadcast(P)).then_inc(s_load["small"], 16)

            def stack(n, par, g):
                dst = qs[:, par, g * R * T:(g + 1) * R * T].bitcast(F32).rearrange("p (i h t) -> p i h t", i=NI, h=R)
                for src, row, ready in ((q_hi, 0, s_q_hi), (q_lo, 2 * L, s_q_lo), (q_hi, L, s_q_hi)):
                    wait(sp, ready, G * n + g + 1)
                    view = src[:, g, :].bitcast(F32).rearrange("p (i t) -> p i t", i=NI)
                    for h in range(R):
                        sp.dma_start(dst[row:row + L, :, h, :], view[h * L:(h + 1) * L]).then_inc(s_qdma[g], 16)

            def stack_max(n, par, g):
                wait(sp, s_nm, NM_STEPS * (G * n + g + 1))
                for part in range(2):
                    dst = qs[K3 + part:K3 + part + 1, par, g * R * T:(g + 1) * R * T].bitcast(F32).rearrange(
                        "p (r t) -> p r t", t=P)
                    sp.dma_start(dst, nmT[part * R * NI:(part + 1) * R * NI, :].bitcast(F32)
                                 ).then_inc(s_mdma[g], 16)

            def load_x(n):
                wait(sp, s_v, n)
                sp.dma_start(x_f[:, 0, :], xT[value(n)]).then_inc(s_x, 16)

            stack(0, 0, 0)
            load_x(1)
            stack(0, 0, 1)
            stack_max(0, 0, 0)
            stack(1, 1, 0)
            sp.wait_ge(s_prep_pe, 2)
            sp.dma_start(raw_lo.rearrange("p (c n) -> p c n", c=FC), h1T).then_inc(s_load["h1"], 16)
            sp.wait_ge(s_prep, PREP_RAW)
            sp.dma_start(raw_hi.rearrange("p (c n) -> p c n", c=FC), h2T).then_inc(s_load["h2"], 16)

            def batch(b, par, before, left):
                if left == 2:
                    load_x(b + 2)
                wait(sp, s_o, b)
                sp.dma_start(x_f[:, 1, :], xT[value(b)]).then_inc(s_x_again, 16)
                stack_max(b, par, 1)
                if left:
                    stack(b + 1, 1 - par, 1)
                    stack_max(b + 1, 1 - par, 0)
                if left == 2:
                    stack(b + 2, par, 0)

            batches(sp, batch)

            def store(t, par, before, left):
                wait(sp, f_y, t + 1)
                sp.dma_start(out[value(t)], y_out[par]).then_inc(f_store[par], 16)

            batches(sp, store)
            for par in range(2):
                sp.wait_ge(f_store[par], 16 * (NB // 2 + 1))

        @block.gpsimd
        def _(pool):
            nc.gpsimd.memset(mean_of[:], 1.0 / P).then_inc(s_const, 1)
            nc.gpsimd.memset(center_f[:], -1.0 / P).then_inc(s_const, 1)
            pool.wait_ge(s_const, 2)
            nc.gpsimd.affine_select(out=center_f[:], in_=center_f[:], compare_op=ALU.not_equal, fill=1.0 - 1.0 / P,
                                    base=0, pattern=[[-1, P]], channel_multiplier=1).then_inc(s_const, 1)
            nc.gpsimd.memset(max_mask[:], 0.0).then_inc(s_const, 1)
            pool.wait_ge(s_const, 4)
            tri = max_mask[:, T - P:T]
            nc.gpsimd.affine_select(out=tri, in_=tri, compare_op=ALU.is_ge, fill=LOWEST,
                                    base=0, pattern=[[-1, P]], channel_multiplier=1).then_inc(s_const, 1)
            nc.gpsimd.memset(vs[:, :, :, :, L:2 * L].rearrange("p a i g l -> p (a i g) l"), 1.0).then_inc(s_const, 1)
            pool.wait_ge(s_const, 6)
            nc.gpsimd.memset(ks[K3:K3M, :, :, :].rearrange("p a g t -> p (a g t)").bitcast(F32),
                             1.0).then_inc(s_const, 1)

            def batch(b, par, before, left):
                for u, (g, i) in enumerate(units):
                    k = items.index((g, i, i))
                    wait(pool, s_exp, NK * b + k + 1)
                    nc.gpsimd.tensor_tensor(gate[:, NX + u:NX + u + 1], mean_of[:, 0:1], mean_of[:, 0:1], ALU.mult)
                    tile = probs[:, k % 4, :]
                    nc.gpsimd.affine_select(out=tile, in_=tile, compare_op=ALU.is_ge, fill=0.0, base=0,
                                            pattern=[[0, R], [1, P]], channel_multiplier=-1).then_inc(s_diag, 1)

            batches(pool, batch)

            pool.wait_ge(s_o, NB)
            nc.gpsimd.memset(three_halves, 1.5).then_inc(s_const, 1)

            def tile(t, par, before, left):
                y, v, h = newton_y[:], newton_t[:], var_half
                wait(pool, f_g, 2 * t + 2)
                for n in range(NEWTON):
                    for m, (dst, a, b, op) in enumerate(((v, y, y, ALU.mult), (v, v, h, ALU.mult),
                                                         (v, v, three_halves, ALU.add), (y, v, y, ALU.mult))):
                        wait(pool, f_n, NEWTON_STEPS * t + 4 * n + m)
                        nc.gpsimd.tensor_tensor(dst, a, b, op).then_inc(f_n, 1)

            pool.wait_ge(s_const, 8)
            batches(pool, tile)

        @block.tensor
        def _(pe):
            mm = nc.tensor.matmul

            def three(dst, w_hi, w_lo, m_hi, m_lo, start=True, stop=True):
                mm(dst, w_hi, m_hi, start=start, stop=False)
                mm(dst, w_lo, m_hi, start=False, stop=False)
                return mm(dst, w_hi, m_lo, start=False, stop=stop)

            pe.wait_ge(s_load["attn"], 16 * (5 + R))
            for h in range(H):
                last = mm(bank_a[:, h * L:(h + 1) * L], wq_raw[:, h, :], wku_f[:], start=True, stop=True)
            last.then_inc(s_prep_pe, 1)
            for h in range(H):
                bank = (bank_max + bank_s)[h // 2]
                last = mm(bank[:, (h % 2) * P:(h % 2 + 1) * P],
                          wvu_f[:].rearrange("p r l -> p (r l)"), wo_raw[:, h, :], start=True, stop=True)
            last.then_inc(s_prep_pe, 1)

            def v_proj(n):
                wait(pe, s_x, 16 * (n + 1))
                if not (isinstance(n, int) and n == 0):
                    wait(pe, s_q_lo, G * n + 1)
                if isinstance(n, int) and n == 0:
                    pe.wait_ge(s_prep, PREP_MQ)
                for j in range(NI):
                    last = mm(bank_a[:, j * G * L:(j + 1) * G * L], x_f[:, 0, j * P:(j + 1) * P], wv_f[:],
                              start=True, stop=True)
                last.then_inc(s_v, 1)

            def q_proj(n, g):
                if isinstance(n, int) and n == 0:
                    wait(pe, *((s_q_lo, 1) if g else (s_v_out, 1)))
                else:
                    wait(pe, *((s_v_out, n + 1) if g else (s_q_lo, G * n)))
                if g == 0:
                    wait(pe, s_x_lo, n + 1)
                w = slice(g * R * L, (g + 1) * R * L)
                three(bank_a[:], mq_hi[:, w], mq_lo[:, w], x_hi[:, 0, :], x_lo[:, 0, :]).then_inc(s_q, 1)

            def k_proj(n, g, before=False):
                if g and before:
                    wait(pe, s_lnv, n - 1)
                else:
                    wait(pe, s_k_lo, G * n + g)
                three(bank_b[0:K3, :], wk_hi[:, g].rearrange("p a l -> p (a l)"),
                      wk_lo[:, g].rearrange("p a l -> p (a l)"), x_hi[:, 0, :],
                      x_lo[:, 0, :]).then_inc(s_k, 1)

            def max_unit(n, par, x):
                if x % XG == 0:
                    g = x // XG
                    wait(pe, s_qdma[g], 16 * 3 * R * (n + 1))
                    wait(pe, s_k_lo, G * n + g + 1)
                if x >= 2 or not (isinstance(n, int) and n == 0):
                    wait(pe, s_mx, NX * n + x - 1)
                for m, (g, i, h) in enumerate(max_units[x]):
                    at = (g * NI * R + i * R + h) * P
                    width = max(256, (i + 1) * P)
                    last = mm(bank_max[x % 2][:, m * 256:m * 256 + width], qs[0:K3, par, at:at + P],
                              ks[0:K3, par, g, 0:width], start=True, stop=True)
                last.then_inc(s_sx, 1)

            v_proj(0)
            q_proj(0, 0)
            q_proj(0, 1)
            k_proj(0, 0)
            k_proj(0, 1)
            pe.wait_ge(s_prep, PREP_WVO)
            q_proj(1, 0)
            k_proj(1, 0)
            for x in range(XG + XL):
                max_unit(0, 0, x)

            def scores(b, par, k):
                g, i, j = items[k % NK]
                if k % NKG == 0:
                    wait(pe, s_mdma[g], 32 * (b + k // NK + 1))
                wait(pe, s_exp, NK * b + k - 1)
                at = (g * NI + i) * R * P
                if k >= NK:
                    par = 1 - par
                mm(bank_s[k % 2][:], ks[0:K3M, par, g, j * P:(j + 1) * P], qs[0:K3M, par, at:at + R * P],
                   start=True, stop=True).then_inc(s_st, 1)

            scores(0, 0, 0)
            scores(0, 0, 1)

            def batch(b, par, before, left):
                for what, k in steps(before, left):
                    if what == "v":
                        v_proj(b + 1)
                    elif what == "o":
                        out_proj(b - 1, 1 - par, left)
                    elif what == "st":
                        scores(b, par, k)
                    elif what == "pv":
                        g, i, j = items[k]
                        u = units.index((g, i))
                        if j == 0:
                            wait(pe, s_y, NU * b + u - 1)
                        if j == i:
                            wait(pe, s_diag, NU * b + u + 1)
                        else:
                            wait(pe, s_exp, NK * b + k + 1)
                        mm(bank_pv[u % 2][0:2 * L, :], vs[:, par, j, g, :], probs[:, k % 4, :],
                           start=(j == 0), stop=(j == i)).then_inc(s_pv, 1)
                    elif what == "q":
                        q_proj(b + k // G, k % G)
                    elif what == "k":
                        k_proj(b + k // G, k % G, before)
                    elif what == "var":
                        var(b - 1)
                    elif what == "mx":
                        if k < NX:
                            max_unit(b, par, k)
                        else:
                            max_unit(b + 1, 1 - par, k - NX)

            def out_proj(n, par, left=None):
                if left is not None:
                    wait(pe, s_k_lo, G * (n + 2) + (1 if left else 0))
                else:
                    wait(pe, s_lnv, n)
                wait(pe, s_x_again, 16 * (n + 1))
                mm(bank_b[:], center_f[:], x_f[:, 1, :], start=True, stop=False)
                wait(pe, s_y, NU * (n + 1))
                for g in range(G):
                    last = mm(bank_b[:], wvo[:, g, :], ys[:, par, g, :], start=False, stop=(g == G - 1))
                last.then_inc(s_o, 1)

            def var(n):
                wait(pe, s_rc, n + 1)
                wait(pe, s_sq, n + 1)
                mm(bank_b[:], mean_of[:], sq[:], start=True, stop=True).then_inc(s_var, 1)

            batches(pe, batch)
            out_proj(NB - 1, (NB - 1) % 2)
            var(NB - 1)

            bank_d, bank_v = bank_a, bank_b
            bank_z = [bank_max, bank_s]
            pe.wait_ge(s_prep, PREP_ALL)
            pe.wait_ge(s_lnv, NB)

            def layer_a(t, par, c):
                if c == 0:
                    wait(pe, f_x_lo, t + 1)
                if c >= 2 or not (isinstance(t, int) and t == 0):
                    wait(pe, f_z, FC * t + c - 1)
                w = slice(c * P, (c + 1) * P)
                three(bank_z[c % 2][0][:], w1_hi[:, w], w1_lo[:, w], x_hi[:, par, :],
                      x_lo[:, par, :]).then_inc(f_a, 1)
                three(bank_z[c % 2][1][:], w2_hi[:, w], w2_lo[:, w], x_hi[:, par, :],
                      x_lo[:, par, :]).then_inc(f_a, 1)

            def layer_h(t, c, w_hi, w_lo, in_hi, in_lo, s_in, s_free, s_done):
                s_free(t, c)
                w = slice(c * P, (c + 1) * P)
                for kc in range(FC):
                    if c == 0:
                        wait(pe, s_in, FC * t + kc + 1)
                    last = three(bank_pv[c % 2][:], w_hi[:, kc, w], w_lo[:, kc, w], in_hi[kc], in_lo[kc],
                                 start=(kc == 0), stop=(kc == FC - 1))
                last.then_inc(s_done, 1)

            def layer_b(t, c):
                def free(t, c):
                    wait(pe, f_cg, FC * t) if c < 2 else wait(pe, f_bg, FC * t + c - 1)
                layer_h(t, c, h1_hi, h1_lo, a_hi, a_lo, f_al, free, f_b)

            def layer_c(t, c):
                def free(t, c):
                    wait(pe, f_bg, FC * (t + 1)) if c < 2 else wait(pe, f_cg, FC * t + c - 1)
                layer_h(t, c, h2_hi, h2_lo, b_hi, b_lo, f_bl, free, f_c)

            def layer_d(t, par):
                wait(pe, f_y, t)
                mm(bank_d[:], center[:], x_hi[:, par, :], start=True, stop=False)
                mm(bank_d[:], center[:], x_lo[:, par, :], start=False, stop=False)
                for kc in range(FC):
                    wait(pe, f_cl, FC * t + kc + 1)
                    last = three(bank_d[:], w3_hi[:, kc, :], w3_lo[:, kc, :], c_hi[kc], c_lo[kc],
                                 start=False, stop=(kc == FC - 1))
                last.then_inc(f_d, 1)

            def f_variance(t):
                wait(pe, f_sq, t + 1)
                wait(pe, f_v, 2 * t)
                mm(bank_v[:], mean_of[:], sq[:], start=True, stop=True).then_inc(f_var, 1)

            for c in range(FC):
                layer_a(0, 0, c)

            def tile(t, par, before, left):
                layer_b(t, 0)
                layer_b(t, 1)
                if before:
                    layer_d(t - 1, 1 - par)
                layer_b(t, 2)
                layer_b(t, 3)
                if before:
                    f_variance(t - 1)
                for layer, c in mlp_order(left):
                    layer_a(t + 1, 1 - par, c) if layer == "a" else layer_c(t, c)

            batches(pe, tile)
            layer_d(NB - 1, (NB - 1) % 2)
            f_variance(NB - 1)

        @block.scalar
        def _(act):
            A = nc.scalar.activation
            nc.scalar.preload_act_table_set("natural_log_exp_and_others")
            act.wait_ge(s_prep_pe, 1)
            A(mq_f[:], bank_a[:, 0:H * L], ACT.Copy, scale=SCALE).then_inc(s_ln, 1)

            def q_evac(n, g):
                wait(act, s_q, G * n + g + 1)
                wait(act, s_qdma[g], 16 * 3 * R * n)
                A(q_hi[:, g, :], bank_a[:], ACT.Copy).then_inc(s_q_hi, 1)

            def k_evac(n, par, g):
                wait(act, s_k, G * n + g + 1)
                wait(act, s_st, NK * (n - 2) + NKG * (g + 1))
                A(ks[0:K3, par, g, :], bank_b[0:K3, :], ACT.Copy).then_inc(s_k_hi, 1)

            for g in range(G):
                q_evac(0, g)
            for g in range(G):
                k_evac(0, 0, g)
            q_evac(1, 0)
            k_evac(1, 1, 0)
            act.wait_ge(s_const, 7)

            def exponentials(b, k):
                wait(act, s_st, NK * b + k + 1)
                wait(act, s_pv, NK * b + k - 3)
                A(probs[:, k % 4, :], bank_s[k % 2][:], ACT.Exp).then_inc(s_exp, 1)

            exponentials(0, 0)
            exponentials(0, 1)

            def batch(b, par, before, left):
                for what, k in steps(before, left):
                    if what == "o":
                        first_norm_a(b - 1)
                    elif what == "st":
                        exponentials(b, k)
                    elif what == "den":
                        denominator(b, k)
                    elif what == "q":
                        q_evac(b + k // G, k % G)
                    elif what == "k":
                        k_evac(b + k // G, par if k // G == 2 else 1 - par, k % G)
                    elif what == "var":
                        first_norm_b(b - 1)

            def denominator(b, u):
                n = u % 2
                ended = 0 if u < 0 else items.index(units[u] + (units[u][1],)) + 1
                wait(act, s_pv, NK * b + ended)
                wait(act, s_y, NU * b + u - 1)
                A(rden[:, n, :], bank_pv[n][L:2 * L, :], ACT.Ln).then_inc(s_ln, 1)
                wait(act, s_ln, NU * b + u + 2)
                A(rden[:, n, :], rden[:, n, :], ACT.Exp, scale=-1.0).then_inc(s_rden, 1)

            def first_norm_a(n):
                wait(act, s_o, n + 1)
                wait(act, s_x1, n)
                A(rc[:], bank_b[:], ACT.Copy).then_inc(s_rc, 1)
                A(sq[:], bank_b[:], ACT.Square).then_inc(s_sq, 1)

            def first_norm_b(n):
                wait(act, s_var, n + 1)
                A(rstd[:], bank_b[:], ACT.Ln, bias=eps_col[:, 0:1]).then_inc(s_lnv, 1)
                wait(act, s_lnv, n + 1)
                A(rstd[:], rstd[:], ACT.Exp, scale=-0.5).then_inc(s_rstd, 1)

            batches(act, batch)
            denominator(NB, -1)
            first_norm_a(NB - 1)
            first_norm_b(NB - 1)

            def a_chunk(t, c):
                n = FC * t + c + 1
                wait(act, f_a, 2 * n)
                wait(act, f_u, n - 2)
                A(t_act[c % 2], (bank_max, bank_s)[c % 2][0][:], ACT.Tanh, scale=s1h[:, c:c + 1]).then_inc(f_t, 1)

            def a_round(t, c):
                n = FC * t + c + 1
                wait(act, f_z, n)
                wait(act, f_b, FC * t)
                A(a_hi[c], u_act[c % 2], ACT.Copy).then_inc(f_ah, 1)

            def gelu(t, c, s_in, scale, hi, s_next, s_used, used, s_done):
                wait(act, s_in, FC * t + c + 1)
                wait(act, s_used, used)
                A(g_act[c % 2], bank_pv[c % 2][:], ACT.Gelu, scale=scale[:, c:c + 1])
                wait(act, s_next[0], s_next[1])
                A(hi[c], bank_pv[c % 2][:], ACT.Gelu, scale=scale[:, c:c + 1]).then_inc(s_done, 1)

            def b_chunk(t, c):
                s_used, used = (f_cl, FC * (t - 1) + c + 3) if c < 2 else (f_bl, FC * t + c - 1)
                gelu(t, c, f_b, sh1, b_hi, (f_c, FC * t), s_used, used, f_bg)

            def c_chunk(t, c):
                s_used, used = (f_bl, FC * t + c + 3) if c < 2 else (f_cl, FC * t + c - 1)
                gelu(t, c, f_c, sh2, c_hi, (f_d, t), s_used, used, f_cg)

            def square(t):
                wait(act, f_d, t + 1)
                wait(act, f_var, t)
                A(sq[:], bank_a[:], ACT.Square).then_inc(f_sq, 1)

            def half_variance(t):
                wait(act, f_var, t + 1)
                wait(act, f_y, t)
                A(var_eps[:], bank_b[:], ACT.Copy, bias=EPS).then_inc(f_v, 1)
                A(var_half, bank_b[:], ACT.Copy, bias=-0.5 * EPS, scale=-0.5).then_inc(f_v, 1)

            nc.scalar.preload_act_table_set("gelu_and_others")
            act.wait_ge(s_prep, PREP_ALL)
            for c in range(FC):
                a_chunk(0, c)
                a_round(0, c)

            def act_step(t, layer, c):
                if layer == "a":
                    a_chunk(t + 1, c)
                    if c:
                        a_round(t + 1, c - 1)
                    if c == FC - 1:
                        a_round(t + 1, c)
                else:
                    c_chunk(t, c)

            def tile(t, par, before, left):
                b_chunk(t, 0)
                b_chunk(t, 1)
                if before:
                    square(t - 1)
                b_chunk(t, 2)
                b_chunk(t, 3)
                if before:
                    half_variance(t - 1)
                for layer, c in mlp_order(left):
                    act_step(t, layer, c)

            batches(act, tile)
            square(NB - 1)
            half_variance(NB - 1)

        @block.vector
        def _(dve):
            V = nc.vector
            count = [0]

            def prep(ins):
                count[0] += 1
                ins.then_inc(s_prep, 1)
                dve.wait_ge(s_prep, count[0])

            def split_weight(hi, lo, raw):
                prep(V.tensor_copy(hi, raw))
                prep(V.tensor_tensor(lo, raw, hi.bitcast(F32), ALU.subtract))

            def split_x(n):
                wait(dve, s_x, 16 * (n + 1))
                wait(dve, s_k, G * n)
                V.tensor_copy(x_hi[:, 0, :], x_f[:, 0, :]).then_inc(s_x_hi, 1)
                wait(dve, s_x_hi, n + 1)
                V.tensor_tensor(x_lo[:, 0, :], x_f[:, 0, :], x_hi[:, 0, :].bitcast(F32),
                                ALU.subtract).then_inc(s_x_lo, 1)

            prep(V.memset(eps_col[:], EPS))
            split_x(0)
            dve.wait_ge(s_load["attn"], 16 * (5 + R))
            for g in range(G):
                raw = wk_f[:, g * L:(g + 1) * L]
                for a in range(3):
                    split_weight(wk_hi[:, g, a, :], wk_lo[:, g, a, :], raw)
            dve.wait_ge(s_ln, 1)
            split_weight(mq_hi[:], mq_lo[:], mq_f[:])
            assert count[0] == PREP_MQ
            dve.wait_ge(s_prep_pe, 2)
            for h in range(H):
                bank = (bank_max + bank_s)[h // 2]
                rows = slice((h % R) * L, (h % R + 1) * L)
                step = V.tensor_copy(wvo[rows, h // R, :], bank[rows, (h % 2) * P:(h % 2 + 1) * P])
                count[0] += 1
                step.then_inc(s_prep, 1)
            dve.wait_ge(s_prep, count[0])
            prep(V.tensor_reduce(wvo_mean[:], wvo[:], AX_X, ALU.add))
            prep(V.tensor_scalar(wvo_mean[:], wvo_mean[:], 1.0 / P, None, ALU.mult))
            for g in range(G):
                prep(V.tensor_scalar(wvo[:, g, :], wvo[:, g, :], wvo_mean[:, g:g + 1], None, ALU.subtract))
            dve.wait_ge(s_const, 7)
            prep(V.tensor_copy(center[:], center_f[:]))
            assert count[0] == PREP_WVO

            def v_evac(n, par):
                wait(dve, s_v, n + 1)
                wait(dve, s_pv, NK * (n - 1))
                V.tensor_copy(vs[:, par, :, :, 0:L].rearrange("p i g l -> p (i g) l"),
                              bank_a[:, 0:NI * G * L].rearrange("p (a l) -> p a l", l=L)).then_inc(s_v_out, 1)

            def q_evac(n, g):
                wait(dve, s_q_hi, G * n + g + 1)
                V.tensor_tensor(q_lo[:, g, :], bank_a[:], q_hi[:, g, :].bitcast(F32), ALU.subtract).then_inc(s_q_lo, 1)

            def k_evac(n, par, g):
                wait(dve, s_k_hi, G * n + g + 1)
                row = ks[L:2 * L, par, g, :]
                V.tensor_tensor(row, bank_b[L:2 * L, :], row.bitcast(F32),
                                ALU.subtract).then_inc(s_k_lo, 1)

            def max_unit(n, x):
                wait(dve, s_sx, NX * n + x + 1)
                V.memset(gate[:, x:x + 1], 0.0)
                for m, (g, i, h) in enumerate(max_units[x]):
                    width = (i + 1) * P
                    scores = bank_max[x % 2][:, m * 256:m * 256 + width]
                    at = g * NI * R + i * R + h
                    last = V.tensor_tensor_reduce(scores, scores, max_mask[:, T - width:T], 1.0, LOWEST, ALU.add,
                                                  ALU.max, mx[:, at:at + 1])
                last.then_inc(s_mx, 1)

            def minus_max(n, g):
                steps_before = NM_STEPS * (G * n + g)
                own = mx[:, g * NI * R:(g + 1) * NI * R]
                wait(dve, s_mx, NX * n + XG * (g + 1))
                V.tensor_scalar(nm[:, 0, :], own, -1.0, None, ALU.mult).then_inc(s_nm, 1)
                wait(dve, s_nm, steps_before + 1)
                V.scalar_tensor_tensor(nm[:, 1, :], own, -1.0, nm[:, 0, :].bitcast(F32), ALU.mult,
                                       ALU.subtract).then_inc(s_nm, 1)
                wait(dve, s_nm, steps_before + 2)
                wait(dve, s_mdma[1 - g], 32 * (n + g))
                for q in range(P // 32):
                    V.transpose(nmT[:, q * 32:(q + 1) * 32].bitcast(F32),
                                nm[q * 32:(q + 1) * 32, :, :].rearrange("p a r -> p (a r)").bitcast(F32)
                                ).then_inc(s_nm, 1)

            v_evac(0, 0)
            for g in range(G):
                q_evac(0, g)
            for g in range(G):
                k_evac(0, 0, g)
            split_x(1)
            q_evac(1, 0)
            k_evac(1, 1, 0)
            for x in range(XG):
                max_unit(0, x)
            minus_max(0, 0)
            for x in range(XG, XG + XL):
                max_unit(0, x)
            dve.wait_ge(s_load["w123"], 48)
            split_weight(w1_hi[:], w1_lo[:], raw_hi[:, 0:F])
            split_weight(w2_hi[:], w2_lo[:], raw_hi[:, F:2 * F])
            dve.wait_ge(s_load["small"], 80)
            w3 = raw_hi[:, 2 * F:3 * F].rearrange("p (c n) -> p c n", c=FC)
            for c in range(FC):
                prep(V.tensor_tensor(w3[:, c, :], w3[:, c, :], s3_row[:], ALU.mult))
            prep(V.tensor_reduce(w3_mean[:], w3, AX_X, ALU.add))
            prep(V.tensor_scalar(w3_mean[:], w3_mean[:], 1.0 / P, None, ALU.mult))
            for c in range(FC):
                prep(V.tensor_scalar(w3[:, c, :], w3[:, c, :], w3_mean[:, c:c + 1], None, ALU.subtract))
            split_weight(w3_hi[:].rearrange("p c n -> p (c n)"), w3_lo[:].rearrange("p c n -> p (c n)"),
                         raw_hi[:, 2 * F:3 * F])
            assert count[0] == PREP_RAW

            def batch(b, par, before, left):
                for what, k in steps(before, left):
                    if what == "v":
                        v_evac(b + 1, 1 - par)
                    elif what == "x":
                        split_x(b + 2)
                    elif what == "q":
                        q_evac(b + k // G, k % G)
                    elif what == "k":
                        k_evac(b + k // G, par if k // G == 2 else 1 - par, k % G)
                    elif what == "var":
                        first_norm(b - 1)
                    elif what == "mx":
                        max_unit(b, k) if k < NX else max_unit(b + 1, k - NX)
                    elif what == "nm":
                        minus_max(b, k) if k < G else minus_max(b + 1, 0)
                    elif what == "y":
                        normalise(b, k, par)

            def normalise(b, u, par):
                g, i = units[u]
                if u < 0:
                    par = 1 - par
                wait(dve, s_rden, NU * b + u + 1)
                wait(dve, s_o, b - 1)
                for h in range(R):
                    last = V.tensor_tensor(ys[h * L:(h + 1) * L, par, g, i * P:(i + 1) * P],
                                           bank_pv[u % 2][0:L, h * P:(h + 1) * P],
                                           rden[:, u % 2, h * P:(h + 1) * P], ALU.mult)
                last.then_inc(s_y, 1)

            def first_norm(n):
                wait(dve, s_rstd, n + 1)
                V.tensor_tensor(x1[:, bass.ds(value(n * T), T)], rc[:], rstd[:], ALU.mult).then_inc(s_x1, 1)

            batches(dve, batch)
            normalise(NB, -1, 0)
            dve.wait_ge(s_load["h1"], 16)
            split_weight(h1_hi[:].rearrange("p c n -> p (c n)"), h1_lo[:].rearrange("p c n -> p (c n)"), raw_lo)
            dve.wait_ge(s_load["h2"], 16)
            split_weight(h2_hi[:].rearrange("p c n -> p (c n)"), h2_lo[:].rearrange("p c n -> p (c n)"), raw_hi)
            prep(V.tensor_scalar(s1h[:], s1h[:], 0.5, None, ALU.mult))
            prep(V.tensor_tensor(s12h[:], s1h[:], s2[:], ALU.mult))
            assert count[0] == PREP_ALL

            first_norm(NB - 1)

            def split_x1(t, par):
                wait(dve, f_d, t - 1)
                if isinstance(t, int) and t == 0:
                    dve.wait_ge(s_x1, NB)
                    dve.wait_ge(s_o, NB)
                source = x1[:, bass.ds(value(t * T), T)]
                V.tensor_copy(x_hi[:, par, :], source).then_inc(f_x_hi, 1)
                wait(dve, f_x_hi, t + 1)
                V.tensor_tensor(x_lo[:, par, :], source, x_hi[:, par, :].bitcast(F32), ALU.subtract).then_inc(f_x_lo, 1)

            def a_chunk(t, c):
                z1, z2 = (bank_max, bank_s)[c % 2]
                n = FC * t + c + 1
                wait(dve, f_t, n)
                wait(dve, f_al, n - 2)
                V.scalar_tensor_tensor(u_act[c % 2], t_act[c % 2], 1.0, z1[:], ALU.add, ALU.mult).then_inc(f_u, 1)
                wait(dve, f_u, n)
                V.scalar_tensor_tensor(u_act[c % 2], z2[:], s12h[:, c:c + 1], u_act[c % 2], ALU.mult,
                                       ALU.mult).then_inc(f_z, 1)

            def a_rest(t, c):
                wait(dve, f_ah, FC * t + c + 1)
                V.tensor_tensor(a_lo[c], u_act[c % 2], a_hi[c].bitcast(F32), ALU.subtract).then_inc(f_al, 1)

            def b_chunk(t, c):
                wait(dve, f_bg, FC * t + c + 1)
                V.tensor_tensor(b_lo[c], g_act[c % 2], b_hi[c].bitcast(F32), ALU.subtract).then_inc(f_bl, 1)

            def c_chunk(t, c):
                wait(dve, f_cg, FC * t + c + 1)
                V.tensor_tensor(c_lo[c], g_act[c % 2], c_hi[c].bitcast(F32), ALU.subtract).then_inc(f_cl, 1)

            def guess(t):
                wait(dve, f_v, 2 * t + 2)
                bits = newton_y[:].bitcast(I32)
                V.tensor_scalar(bits, var_eps[:].bitcast(I32), 1, None, ALU.logical_shift_right).then_inc(f_g, 1)
                wait(dve, f_g, 2 * t + 1)
                V.tensor_scalar(bits, bits, -1.0, float(RSQRT_MAGIC), ALU.mult, ALU.add).then_inc(f_g, 1)

            def second_norm(t, par):
                wait(dve, f_n, NEWTON_STEPS * (t + 1))
                wait(dve, f_store[par], 8 * (t - par) + 16)
                V.tensor_tensor(y_out[par], bank_a[:], newton_y[:], ALU.mult).then_inc(f_y, 1)

            for par in range(2):
                V.memset(gate[:, par:par + 1], 0.0).then_inc(f_store[par], 16)
            split_x1(0, 0)
            for c in range(FC):
                a_chunk(0, c)
                a_rest(0, c)

            def tile(t, par, before, left):
                b_chunk(t, 0)
                b_chunk(t, 1)
                if left:
                    split_x1(t + 1, 1 - par)
                b_chunk(t, 2)
                b_chunk(t, 3)
                if before:
                    guess(t - 1)
                for layer, c in mlp_order(left):
                    if layer == "a":
                        a_chunk(t + 1, c)
                        if c:
                            a_rest(t + 1, c - 1)
                        if c == FC - 1:
                            a_rest(t + 1, c)
                    else:
                        c_chunk(t, c)
                if before:
                    second_norm(t - 1, 1 - par)

            batches(dve, tile)
            guess(NB - 1)
            second_norm(NB - 1, (NB - 1) % 2)


def kernel(**inputs):
    import numpy as np
    import concourse.bacc as bacc
    from concourse.bass_utils import run_bass_kernel_spmd

    a = {n: np.asarray(v) for n, v in inputs.items()}
    NB, T, D = a["L0_attn_x"].shape
    HD = a["L0_attn_wk_up"].shape[1]
    H = a["L0_attn_wq"].shape[1] // HD
    F = a["L0_ffn_w1_w"].shape[0]
    FC = F // P

    def columns(s):
        return s.reshape(FC, P).T

    def wide(w):
        return w.T.reshape(w.shape[1] // P, P, w.shape[0]).transpose(1, 0, 2)

    laid = {
        "xT": a["L0_attn_x"].transpose(0, 2, 1),
        "wqT": a["L0_attn_wq"].reshape(D, H, HD).transpose(2, 1, 0),
        "wk_down": a["L0_attn_wk_down"],
        "wv_down": a["L0_attn_wv_down"],
        "wk_upT": a["L0_attn_wk_up"].T,
        "wv_upT": a["L0_attn_wv_up"].T,
        "wo": a["L0_attn_wo"].reshape(H, HD, D).transpose(1, 0, 2),
        "w1T": a["L0_ffn_w1_w"].T,
        "w1_s": columns(a["L0_ffn_w1_s"]),
        "w2T": a["L0_ffn_w2_w"].T,
        "w2_s": columns(a["L0_ffn_w2_s"]),
        "h1T": wide(a["L0_ffn_h1_w"]),
        "h1_s": columns(a["L0_ffn_h1_s"]),
        "h2T": wide(a["L0_ffn_h2_w"]),
        "h2_s": columns(a["L0_ffn_h2_s"]),
        "w3T": wide(a["L0_ffn_w3_w"]),
        "w3_s": a["L0_ffn_w3_s"],
    }
    laid = {n: np.ascontiguousarray(v) for n, v in laid.items()}
    nc = bacc.Bacc("TRN2", target_bir_lowering=False, num_devices=1)
    args = {n: nc.dram_tensor(f"{n}_dram", v.shape, F32, kind="ExternalInput").ap() for n, v in laid.items()}
    args["out"] = nc.dram_tensor("out_dram", (NB, D, T), F32, kind="ExternalOutput").ap()
    build_layer(nc, **args)
    r = run_bass_kernel_spmd(nc, [{f"{n}_dram": v for n, v in laid.items()}], core_ids=[0])
    return np.ascontiguousarray(r.results[0]["out_dram"].transpose(0, 2, 1))
```

```python
from contextlib import ExitStack

import concourse.bass as bass
from concourse import mybir

F32 = mybir.dt.float32
F32R = mybir.dt.float32r
I32 = mybir.dt.int32
ALU = mybir.AluOpType
ACT = mybir.ActivationFunctionType
AX_X = mybir.AxisListType.X

P = 128
LOWEST = -3.0e38
EPS = 1e-5
RSQRT_MAGIC = 0x5F3759DF
NEWTON = 3


class Count:

    def __init__(self, reg, mul=1, add=0):
        self.reg, self.mul, self.add = reg, mul, add

    def __add__(self, n):
        return Count(self.reg, self.mul, self.add + n)

    def __sub__(self, n):
        return self + -n

    def __mul__(self, n):
        return Count(self.reg, self.mul * n, self.add * n)

    __radd__, __rmul__ = __add__, __mul__

    def value(self):
        return (self.reg * self.mul if self.mul != 1 else self.reg) + self.add if self.add else self.reg * self.mul


def value(n):
    return n.value() if isinstance(n, Count) else n


def build_layer(nc, xT, wqT, wk_down, wv_down, wk_upT, wv_upT, wo, w1T, w1_s, w2T, w2_s, h1T, h1_s, h2T, h2_s, w3T,
                w3_s, out):
    NB, D, T = xT.shape
    HD, H, _ = wqT.shape
    L = wk_upT.shape[1]
    G = wk_down.shape[1] // L
    R = H // G
    F = w1T.shape[1]
    FC = F // P
    NI = T // P
    K3 = 3 * L
    K3M = K3 + 2
    SCALE = float(HD) ** -0.5
    PREP_MQ = 1 + 2 * 3 * G + 2
    PREP_WVO = PREP_MQ + H + 2 + G + 2
    PREP_RAW = PREP_WVO + 4 + 2 * FC + 2 + 2
    PREP_WIDE = PREP_RAW + 4 * FC + 2 + 2 * FC + 2
    PREP_ALL = PREP_WIDE + 2 + 1
    NM_STEPS = 2 + P // 32
    NEWTON_STEPS = 4 * NEWTON
    assert D == P and HD == P and FC == 2 * G and T == 512 and R * L == P and 2 * R * NI == 32
    assert G == 2 and NB % 2 == 0 and NB > 4

    items = [(g, i, j) for g in range(G) for i in range(NI) for j in range(i + 1)]
    NK = len(items)
    units = [(g, i) for g in range(G) for i in range(NI)]
    NU = len(units)
    last_of_unit = {items.index((g, i, i)): u for u, (g, i) in enumerate(units)}
    max_units = [[(g, i, h) for h in range(h0, h0 + (2 if i < 2 else 1))]
                 for g in range(G) for i in range(NI) for h0 in range(0, R, 2 if i < 2 else 1)]
    NX = len(max_units)
    XG = NX // G
    NKG = NK // G
    max_at = [2, 1, 1, 2, 1, 1, 1, 1, 1, 1]
    NM_AT = 3
    OUT_AT, SQUARE_AT, VAR_AT, RSTD_AT, NORM_AT = 4, 5, 7, 8, 9
    Q_AT, K_AT, X_AT, X_AGAIN_AT = 5, 7, 10, 13
    XL = sum(max_at[NM_AT + 1:])
    assert len(max_at) == NKG and sum(max_at) == XG

    with ExitStack() as ctx:
        def sb(name, shape, dt=F32):
            return ctx.enter_context(nc.sbuf_tensor(name, shape, dt))

        def pb(name, shape=(P, 512)):
            return ctx.enter_context(nc.psum_tensor(name, list(shape), F32))

        def sem(name):
            return ctx.enter_context(nc.semaphore(name))

        mq_f = sb("mq_f", [P, H * L])
        mq_hi = sb("mq_hi", [P, H * L], F32R)
        mq_lo = sb("mq_lo", [P, H * L], F32R)
        wk_f = sb("wk_f", [P, G * L])
        wk_hi = sb("wk_hi", [P, G, 3, L], F32R)
        wk_lo = sb("wk_lo", [P, G, 3, L], F32R)
        wv_f = sb("wv_f", [P, G * L])
        wku_f = sb("wku_f", [P, L])
        wvu_f = sb("wvu_f", [P, R, L])
        wvo = sb("wvo", [P, G, P])
        wvo_mean = sb("wvo_mean", [P, G])
        w1_hi, w1_lo = sb("w1_hi", [P, F], F32R), sb("w1_lo", [P, F], F32R)
        w2_hi, w2_lo = sb("w2_hi", [P, F], F32R), sb("w2_lo", [P, F], F32R)
        h1_hi, h1_lo = sb("h1_hi", [P, FC, F], F32R), sb("h1_lo", [P, FC, F], F32R)
        h2_hi, h2_lo = sb("h2_hi", [P, FC, F], F32R), sb("h2_lo", [P, FC, F], F32R)
        w3_hi, w3_lo = sb("w3_hi", [P, FC, P], F32R), sb("w3_lo", [P, FC, P], F32R)
        w3_mean = sb("w3_mean", [P, FC])
        s1h = sb("s1h", [P, FC])
        s12h = sb("s12h", [P, FC])
        s2 = sb("s2", [P, FC])
        sh1 = sb("sh1", [P, FC])
        sh2 = sb("sh2", [P, FC])
        s3_row = sb("s3_row", [P, P])
        center_f = sb("center_f", [P, P])
        center = sb("center", [P, P], F32R)
        mean_of = sb("mean_of", [P, P])
        mean_exact = sb("mean_exact", [P, P], F32R)
        unit_128 = sb("unit_128", [P, P])
        max_mask = sb("max_mask", [P, T])
        x_f = sb("x_f", [P, 2, T])
        x_hi = sb("x_hi", [P, 2, T], F32R)
        x_lo = sb("x_lo", [P, 2, T], F32R)
        q_hi = sb("q_hi", [P, G, T], F32R)
        q_lo = sb("q_lo", [P, G, T], F32R)
        qs = sb("qs", [P, 2, H * T], F32R)
        ks = sb("ks", [P, 2, G, T], F32R)
        vs = sb("vs", [P, 2, NI, G, 2 * L])
        probs = sb("probs", [P, 4, T])
        rden = sb("rden", [L, 2, T])
        ys = sb("ys", [P, 2, G, T])
        mx = sb("mx", [P, H * NI])
        nm = sb("nm", [P, 2, R * NI], F32R)
        nmT = sb("nmT", [2 * R * NI, P], F32R)
        rc = sb("rc", [P, T])
        sq = sb("sq", [P, T])
        sq_hi, sq_lo = sb("sq_hi", [P, T], F32R), sb("sq_lo", [P, T], F32R)
        rstd = sb("rstd", [P, T])
        x1 = sb("x1", [P, NB * T])
        eps_col = sb("eps_col", [P, 1])
        gate = sb("gate", [P, NX + NU])
        tmp = sb("tmp", [P, 8, T])
        c_act = sb("c_act", [P, FC * T], F32R)
        a_hi = [qs[:, 0, c * T:(c + 1) * T] for c in range(FC)]
        a_lo = [qs[:, 0, (FC + c) * T:(FC + c + 1) * T] for c in range(FC)]
        b_hi = [qs[:, 1, c * T:(c + 1) * T] for c in range(FC)]
        b_lo = [qs[:, 1, (FC + c) * T:(FC + c + 1) * T] for c in range(FC)]
        c_hi = [(q_hi, q_lo)[c // G][:, c % G, :] for c in range(FC)]
        c_lo = [c_act[:, c * T:(c + 1) * T] for c in range(FC)]
        raw_lo = tmp[:, 0:4, :].rearrange("p a n -> p (a n)")
        raw_hi = tmp[:, 4:8, :].rearrange("p a n -> p (a n)")
        wq_raw = raw_lo[:, 0:H * P].rearrange("p (h d) -> p h d", h=H)
        wo_raw = raw_lo[:, H * P:2 * H * P].rearrange("p (h d) -> p h d", h=H)
        t_act = [tmp[:, n, :] for n in range(2)]
        u_act = [probs[:, c, :] for c in range(FC)]
        g_act = [tmp[:, 4 + n, :] for n in range(2)]
        y_out = [tmp[:, 6 + n, :] for n in range(2)]
        var_eps, var_half = sb("var_eps", [P, NI]), sb("var_half", [P, NI])
        newton_y, newton_t, three_halves = sb("newton_y", [P, NI]), sb("newton_t", [P, NI]), sb("three_halves", [P, NI])
        y_hi, y_lo = sb("y_hi", [P, NI], F32R), sb("y_lo", [P, NI], F32R)
        diag_hi, diag_lo = sq_hi, sq_lo
        low_parts = sb("low_parts", [P, 2 + 2 * FC])
        has_low = sb("has_low", [P, 1])
        inexact = sb("inexact", [1, 1], I32)

        bank_a, bank_b = pb("bank_a"), pb("bank_b")
        bank_max = [pb("bank_max0"), pb("bank_max1")]
        bank_s = [pb("bank_s0"), pb("bank_s1")]
        bank_pv = [pb("bank_pv0"), pb("bank_pv1")]

        long_units = [u for u, (g, i) in enumerate(units) if i]

        def bank_of(u):
            return bank_pv[long_units.index(u) % 2] if u in long_units else bank_b

        def last_in_bank(u):
            w = long_units.index(u)
            return long_units[w - 2] - (NU if w < 2 else 0)

        s_load = {n: sem(f"s_load_{n}") for n in ("query", "attn", "small", "w123", "h1", "h2")}
        s_x = sem("s_x")
        s_x_again = sem("s_x_again")
        s_const = sem("s_const")
        s_prep_pe = sem("s_prep_pe")
        s_prep = sem("s_prep")
        s_x_hi, s_x_lo = sem("s_x_hi"), sem("s_x_lo")
        s_again_hi, s_again_lo = sem("s_again_hi"), sem("s_again_lo")
        s_v, s_q, s_k = sem("s_v"), sem("s_q"), sem("s_k")
        s_v_out = sem("s_v_out")
        s_q_hi, s_q_lo = sem("s_q_hi"), sem("s_q_lo")
        s_k_hi, s_k_lo = sem("s_k_hi"), sem("s_k_lo")
        s_qdma = [sem(f"s_qdma{g}") for g in range(G)]
        s_sx = sem("s_sx")
        s_mx = sem("s_mx")
        s_nm = sem("s_nm")
        s_mdma = [sem(f"s_mdma{g}") for g in range(G)]
        s_st = sem("s_st")
        s_exp = sem("s_exp")
        s_diag = sem("s_diag")
        s_pv = sem("s_pv")
        s_ln, s_rden = sem("s_ln"), sem("s_rden")
        s_y = sem("s_y")
        s_o, s_rc, s_sq, s_sq_lo, s_var = sem("s_o"), sem("s_rc"), sem("s_sq"), sem("s_sq_lo"), sem("s_var")
        s_lnv, s_rstd, s_x1 = sem("s_lnv"), sem("s_rstd"), sem("s_x1")
        f_x_hi, f_x_lo = sem("f_x_hi"), sem("f_x_lo")
        f_a, f_b, f_c, f_d = sem("f_a"), sem("f_b"), sem("f_c"), sem("f_d")
        f_t = sem("f_t")
        f_u, f_z, f_ah, f_al = sem("f_u"), sem("f_z"), sem("f_ah"), sem("f_al")
        f_bg, f_bl, f_cg, f_cl = sem("f_bg"), sem("f_bl"), sem("f_cg"), sem("f_cl")
        f_sq, f_var, f_v, f_g, f_n = sem("f_sq"), sem("f_var"), sem("f_v"), sem("f_g"), sem("f_n")
        f_yh, f_i, f_w, f_r, f_y = sem("f_yh"), sem("f_i"), sem("f_w"), sem("f_r"), sem("f_y")
        f_store = [sem("f_store0"), sem("f_store1")]

        def wait(eng, s, n):
            if not isinstance(n, int) or n > 0:
                eng.wait_ge(s, value(n))

        def batches(eng, body):
            body(0, 0, False, 2)
            body(1, 1, True, 2)
            with eng.Fori(2, NB - 3, 2) as reg:
                b = Count(reg)
                body(b, 0, True, 2)
                body(b + 1, 1, True, 2)
            body(NB - 2, 0, True, 1)
            body(NB - 1, 1, True, 0)

        def steps(before, left):
            seq = []
            if left:
                seq.append(("v", 1))
            nx = XG + XL
            for k in range(NK):
                ended = last_of_unit.get((k - 1) % NK)
                if ended is not None and k == 0:
                    ended = -1 if before else None
                if ended is not None:
                    seq.append(("den", ended))
                if k + 2 < NK or left:
                    seq.append(("st", k + 2))
                seq.append(("pv", k))
                for what, at in (("o", OUT_AT), ("sqr", SQUARE_AT), ("var", VAR_AT), ("rstd", RSTD_AT),
                                 ("norm", NORM_AT)):
                    if k == at and before:
                        seq.append((what, -1))
                if k == Q_AT and left:
                    seq.append(("q", 1 * G + 1))
                if k == K_AT and left:
                    seq.append(("k", 1 * G + 1))
                if k == X_AGAIN_AT:
                    seq.append(("xr", 0))
                if k == X_AT and left == 2:
                    seq.append(("x", 2))
                if k == NKG + Q_AT and left == 2:
                    seq.append(("q", 2 * G))
                if k == NKG + K_AT and left == 2:
                    seq.append(("k", 2 * G))
                for _ in range(max_at[k % NKG]):
                    if nx < NX or left:
                        seq.append(("mx", nx))
                        nx += 1
                if ended is not None:
                    seq.append(("y", ended))
                if k % NKG == NM_AT and (k < NKG or left):
                    seq.append(("nm", k // NKG + 1))
            return seq

        def two_before(t):
            return not isinstance(t, int) or t >= 2

        def mlp_order(left):
            a = [("a", c) for c in range(FC)] if left else []
            c = [("c", c) for c in range(FC)]
            return a[0:2] + c[0:1] + a[2:3] + c[1:2] + a[3:4] + c[2:]

        block = ctx.enter_context(nc.Block())

        @block.sync
        def _(sp):
            sp.dma_start(x_f[:, 0, :], xT[0]).then_inc(s_x, 16)
            sp.dma_start(wq_raw, wqT).then_inc(s_load["query"], 16)
            sp.dma_start(wku_f[:], wk_upT).then_inc(s_load["query"], 16)
            sp.dma_start(wk_f[:], wk_down).then_inc(s_load["attn"], 16)
            sp.dma_start(wv_f[:], wv_down).then_inc(s_load["attn"], 16)
            sp.dma_start(wo_raw, wo).then_inc(s_load["attn"], 16)
            for r in range(R):
                sp.dma_start(wvu_f[:, r, :], wv_upT).then_inc(s_load["attn"], 16)
            sp.dma_start(raw_hi[:, 0:F], w1T).then_inc(s_load["w123"], 16)
            sp.dma_start(raw_hi[:, F:2 * F], w2T).then_inc(s_load["w123"], 16)
            sp.dma_start(raw_hi[:, 2 * F:3 * F].rearrange("p (c n) -> p c n", c=FC), w3T).then_inc(s_load["w123"], 16)
            for dst, src in ((s1h, w1_s), (s2, w2_s), (sh1, h1_s), (sh2, h2_s)):
                sp.dma_start(dst[:], src).then_inc(s_load["small"], 16)
            sp.dma_start(s3_row[:], w3_s.partition_broadcast(P)).then_inc(s_load["small"], 16)

            def stack(n, par, g):
                for src, row, ready in ((q_hi, 0, s_q_hi), (q_lo, 2 * L, s_q_lo), (q_hi, L, s_q_hi)):
                    wait(sp, ready, G * n + g + 1)
                    for h in range(R):
                        at = (g * R + h) * T
                        sp.dma_start(qs[row:row + L, par, at:at + T].bitcast(F32),
                                     src[h * L:(h + 1) * L, g, :].bitcast(F32)).then_inc(s_qdma[g], 16)

            def stack_max(n, par, g):
                wait(sp, s_nm, NM_STEPS * (G * n + g + 1))
                for part in range(2):
                    dst = qs[K3 + part:K3 + part + 1, par, g * R * T:(g + 1) * R * T].bitcast(F32).rearrange(
                        "p (r t) -> p r t", t=P)
                    sp.dma_start(dst, nmT[part * R * NI:(part + 1) * R * NI, :].bitcast(F32)
                                 ).then_inc(s_mdma[g], 16)

            def load_x(n):
                wait(sp, s_v, n)
                sp.dma_start(x_f[:, 0, :], xT[value(n)]).then_inc(s_x, 16)

            load_x(1)
            stack(0, 0, 0)
            stack(0, 0, 1)
            stack_max(0, 0, 0)
            stack(1, 1, 0)
            sp.wait_ge(s_prep_pe, 2)
            sp.dma_start(raw_lo.rearrange("p (c n) -> p c n", c=FC), h1T).then_inc(s_load["h1"], 16)

            def batch(b, par, before, left):
                if left == 2:
                    load_x(b + 2)
                wait(sp, s_again_lo, b)
                sp.dma_start(x_f[:, 1, :], xT[value(b)]).then_inc(s_x_again, 16)
                stack_max(b, par, 1)
                if isinstance(b, int) and b == 1:
                    sp.wait_ge(s_prep, PREP_RAW)
                    sp.dma_start(raw_hi.rearrange("p (c n) -> p c n", c=FC), h2T).then_inc(s_load["h2"], 16)
                if left:
                    stack(b + 1, 1 - par, 1)
                    stack_max(b + 1, 1 - par, 0)
                if left == 2:
                    stack(b + 2, par, 0)

            batches(sp, batch)

            def store(t, par, before, left):
                wait(sp, f_y, t + 1)
                sp.dma_start(out[value(t)], y_out[par]).then_inc(f_store[par], 16)

            batches(sp, store)
            for par in range(2):
                sp.wait_ge(f_store[par], 16 * (NB // 2 + 1))

        @block.gpsimd
        def _(pool):
            nc.gpsimd.memset(mean_of[:], 1.0 / P).then_inc(s_const, 1)
            nc.gpsimd.memset(center_f[:], -1.0 / P).then_inc(s_const, 1)
            pool.wait_ge(s_const, 2)
            nc.gpsimd.affine_select(out=center_f[:], in_=center_f[:], compare_op=ALU.not_equal, fill=1.0 - 1.0 / P,
                                    base=0, pattern=[[-1, P]], channel_multiplier=1).then_inc(s_const, 1)
            nc.gpsimd.memset(max_mask[:], 0.0).then_inc(s_const, 1)
            pool.wait_ge(s_const, 4)
            tri = max_mask[:, T - P:T]
            nc.gpsimd.affine_select(out=tri, in_=tri, compare_op=ALU.is_ge, fill=LOWEST,
                                    base=0, pattern=[[-1, P]], channel_multiplier=1).then_inc(s_const, 1)
            nc.gpsimd.memset(vs[:, :, :, :, L:2 * L].rearrange("p a i g l -> p (a i g) l"), 1.0).then_inc(s_const, 1)
            pool.wait_ge(s_const, 6)
            nc.gpsimd.memset(ks[K3:K3M, :, :, :].rearrange("p a g t -> p (a g t)").bitcast(F32),
                             1.0).then_inc(s_const, 1)
            pool.wait_ge(s_const, 7)
            nc.gpsimd.memset(unit_128[:], 0.0).then_inc(s_const, 1)
            pool.wait_ge(s_const, 8)
            nc.gpsimd.affine_select(out=unit_128[:], in_=unit_128[:], compare_op=ALU.not_equal, fill=float(P),
                                    base=0, pattern=[[-1, P]], channel_multiplier=1).then_inc(s_const, 1)
            nc.gpsimd.memset(three_halves[:], 1.5).then_inc(s_const, 1)

            def square_rest(n):
                wait(pool, s_sq, 2 * n + 2)
                nc.gpsimd.tensor_tensor(sq_lo[:], sq[:], sq_hi[:].bitcast(F32), ALU.subtract).then_inc(s_sq_lo, 1)

            def causal(b, k):
                u = last_of_unit[k % NK]
                wait(pool, s_exp, NK * b + k + 1)
                nc.gpsimd.tensor_tensor(gate[:, NX + u:NX + u + 1], mean_of[:, 0:1], mean_of[:, 0:1], ALU.mult)
                tile = probs[:, k % 4, :]
                nc.gpsimd.affine_select(out=tile, in_=tile, compare_op=ALU.is_ge, fill=0.0, base=0,
                                        pattern=[[0, R], [1, P]], channel_multiplier=-1).then_inc(s_diag, 1)

            def batch(b, par, before, left):
                for what, k in steps(before, left):
                    if what == "sqr":
                        square_rest(b - 1)
                    elif what == "x":
                        wait(pool, s_x_hi, b + 3)
                        nc.gpsimd.tensor_tensor(x_lo[:, 0, :], x_f[:, 0, :], x_hi[:, 0, :].bitcast(F32),
                                                ALU.subtract).then_inc(s_x_lo, 1)
                    elif what == "xr":
                        wait(pool, s_again_hi, b + 1)
                        nc.gpsimd.tensor_tensor(x_lo[:, 1, :], x_f[:, 1, :], x_hi[:, 1, :].bitcast(F32),
                                                ALU.subtract).then_inc(s_again_lo, 1)
                    elif what == "st" and k % NK in last_of_unit:
                        causal(b, k)

            causal(0, 0)
            batches(pool, batch)
            square_rest(NB - 1)

            def newton(t, n):
                y, v, h = newton_y[:], newton_t[:], var_half[:]
                if n == 0:
                    wait(pool, f_g, 2 * t + 2)
                for m, (dst, a, b, op) in enumerate(((v, y, y, ALU.mult), (v, v, h, ALU.mult),
                                                     (v, v, three_halves[:], ALU.add), (y, v, y, ALU.mult))):
                    wait(pool, f_n, NEWTON_STEPS * t + 4 * n + m)
                    nc.gpsimd.tensor_tensor(dst, a, b, op).then_inc(f_n, 1)

            def a_rest(t, c):
                wait(pool, f_ah, FC * t + c + 1)
                nc.gpsimd.tensor_tensor(a_lo[c], u_act[c], a_hi[c].bitcast(F32), ALU.subtract).then_inc(f_al, 1)

            pool.wait_ge(s_const, 10)
            for c in range(FC):
                a_rest(0, c)

            def tile(t, par, before, left):
                if before:
                    for n in range(NEWTON):
                        newton(t - 1, n)
                if left:
                    for c in range(FC):
                        a_rest(t + 1, c)

            batches(pool, tile)
            for n in range(NEWTON):
                newton(NB - 1, n)

        @block.tensor
        def _(pe):
            mm = nc.tensor.matmul

            def three(dst, w_hi, w_lo, m_hi, m_lo, start=True, stop=True):
                mm(dst, w_hi, m_hi, start=start, stop=False)
                mm(dst, w_lo, m_hi, start=False, stop=False)
                return mm(dst, w_hi, m_lo, start=False, stop=stop)

            pe.wait_ge(s_load["query"], 32)
            for h in range(H):
                last = mm(bank_a[:, h * L:(h + 1) * L], wq_raw[:, h, :], wku_f[:], start=True, stop=True)
            last.then_inc(s_prep_pe, 1)
            pe.wait_ge(s_load["attn"], 16 * (3 + R))
            for h in range(H):
                bank = (bank_max + bank_s)[h // 2]
                last = mm(bank[:, (h % 2) * P:(h % 2 + 1) * P],
                          wvu_f[:].rearrange("p r l -> p (r l)"), wo_raw[:, h, :], start=True, stop=True)
            last.then_inc(s_prep_pe, 1)

            def v_proj(n):
                wait(pe, s_x, 16 * (n + 1))
                if not (isinstance(n, int) and n == 0):
                    wait(pe, s_k_lo, G * n + 1)
                if isinstance(n, int) and n == 0:
                    pe.wait_ge(s_prep, PREP_MQ)
                for j in range(NI):
                    last = mm(bank_a[:, j * G * L:(j + 1) * G * L], x_f[:, 0, j * P:(j + 1) * P], wv_f[:],
                              start=True, stop=True)
                last.then_inc(s_v, 1)

            def q_proj(n, g):
                if isinstance(n, int) and n == 0:
                    wait(pe, *((s_k_lo, 1) if g else (s_v_out, 1)))
                else:
                    wait(pe, *((s_v_out, n + 1) if g else (s_k_lo, G * n)))
                if g == 0:
                    wait(pe, s_x_lo, n + 1)
                w = slice(g * R * L, (g + 1) * R * L)
                three(bank_a[:], mq_hi[:, w], mq_lo[:, w], x_hi[:, 0, :], x_lo[:, 0, :]).then_inc(s_q, 1)

            def k_proj(n, g):
                wait(pe, s_q_lo, G * n + g + 1)
                three(bank_a[0:K3, :], wk_hi[:, g].rearrange("p a l -> p (a l)"),
                      wk_lo[:, g].rearrange("p a l -> p (a l)"), x_hi[:, 0, :],
                      x_lo[:, 0, :]).then_inc(s_k, 1)

            def max_unit(n, par, x):
                if x % XG == 0:
                    g = x // XG
                    wait(pe, s_qdma[g], 16 * 3 * R * (n + 1))
                    wait(pe, s_k_lo, G * n + g + 1)
                if x >= 2 or not (isinstance(n, int) and n == 0):
                    wait(pe, s_mx, NX * n + x - 1)
                for m, (g, i, h) in enumerate(max_units[x]):
                    at = ((g * R + h) * NI + i) * P
                    width = max(256, (i + 1) * P)
                    last = mm(bank_max[x % 2][:, m * 256:m * 256 + width], qs[0:K3, par, at:at + P],
                              ks[0:K3, par, g, 0:width], start=True, stop=True)
                last.then_inc(s_sx, 1)

            v_proj(0)
            q_proj(0, 0)
            k_proj(0, 0)
            q_proj(0, 1)
            k_proj(0, 1)
            q_proj(1, 0)
            k_proj(1, 0)
            pe.wait_ge(s_prep, PREP_WVO)
            for x in range(XG + XL):
                max_unit(0, 0, x)

            def scores(b, par, k):
                g, i, j = items[k % NK]
                if k % NKG == 0:
                    wait(pe, s_mdma[g], 32 * (b + k // NK + 1))
                wait(pe, s_exp, NK * b + k - 1)
                if k >= NK:
                    par = 1 - par
                heads = qs[0:K3M, par, g * R * T:(g + 1) * R * T].rearrange("p (h t) -> p h t", h=R)
                mm(bank_s[k % 2][:].rearrange("p (h t) -> p h t", h=R), ks[0:K3M, par, g, j * P:(j + 1) * P],
                   heads[:, :, i * P:(i + 1) * P], start=True, stop=True).then_inc(s_st, 1)

            scores(0, 0, 0)
            scores(0, 0, 1)

            def batch(b, par, before, left):
                if isinstance(b, int) and b == NB - 1:
                    pe.wait_ge(s_prep, PREP_WIDE)
                    mm(bank_a[0:1, 0:1], has_low[:], mean_of[:, 0:1], start=True, stop=True).then_inc(s_prep_pe, 1)
                for what, k in steps(before, left):
                    if what == "v":
                        v_proj(b + 1)
                    elif what == "o":
                        out_proj(b - 1, 1 - par, NU * b + 1)
                    elif what == "st":
                        scores(b, par, k)
                    elif what == "pv":
                        g, i, j = items[k]
                        u = units.index((g, i))
                        if u in long_units and j == 0:
                            wait(pe, s_y, NU * b + last_in_bank(u) + 1)
                        elif j == 0 and g and before:
                            wait(pe, s_lnv, b)
                        elif j == 0 and (g or before):
                            wait(pe, s_y, NU * b + (u if g else 0) - NI + 1)
                        if j == i:
                            wait(pe, s_diag, NU * b + u + 1)
                        else:
                            wait(pe, s_exp, NK * b + k + 1)
                        mm(bank_of(u)[0:2 * L, :], vs[:, par, j, g, :], probs[:, k % 4, :],
                           start=(j == 0), stop=(j == i)).then_inc(s_pv, 1)
                    elif what == "q":
                        q_proj(b + k // G, k % G)
                    elif what == "k":
                        k_proj(b + k // G, k % G)
                    elif what == "var":
                        var(b - 1)
                    elif what == "mx":
                        if k < NX:
                            max_unit(b, par, k)
                        else:
                            max_unit(b + 1, 1 - par, k - NX)

            def out_proj(n, par, n_units=None):
                if n_units is not None:
                    wait(pe, s_y, n_units)
                wait(pe, s_again_lo, n + 1)
                mm(bank_b[:], center[:], x_hi[:, 1, :], start=True, stop=False)
                mm(bank_b[:], center[:], x_lo[:, 1, :], start=False, stop=False)
                wait(pe, s_y, NU * (n + 1))
                for g in range(G):
                    last = mm(bank_b[:], wvo[:, g, :], ys[:, par, g, :], start=False, stop=(g == G - 1))
                last.then_inc(s_o, 1)

            def var(n):
                wait(pe, s_rc, n + 1)
                wait(pe, s_sq_lo, n + 1)
                mm(bank_b[:], mean_exact[:], sq_hi[:], start=True, stop=False)
                mm(bank_b[:], mean_exact[:], sq_lo[:], start=False, stop=True).then_inc(s_var, 1)

            batches(pe, batch)

            bank_d, bank_v = bank_a, bank_b
            bank_z = [bank_max, bank_s]
            pe.wait_ge(s_prep, PREP_ALL)
            some_low = pe.value_load(inexact[0:1, 0:1], min_val=0, max_val=1)
            exact_weights = [False]

            def layer(dst, w_hi, w_lo, m_hi, m_lo, start=True, stop=True):
                if exact_weights[0]:
                    mm(dst, w_hi, m_hi, start=start, stop=False)
                    return mm(dst, w_hi, m_lo, start=False, stop=stop)
                return three(dst, w_hi, w_lo, m_hi, m_lo, start=start, stop=stop)

            def layer_a(t, par, c):
                if c == 0:
                    wait(pe, f_x_lo, t + 1)
                if c >= 2 or not (isinstance(t, int) and t == 0):
                    wait(pe, f_z, FC * t + c - 1)
                elif c == 1:
                    pe.wait_ge(s_exp, NK * NB)
                w = slice(c * P, (c + 1) * P)
                layer(bank_z[c % 2][0][:], w1_hi[:, w], w1_lo[:, w], x_hi[:, par, :],
                      x_lo[:, par, :]).then_inc(f_a, 1)
                layer(bank_z[c % 2][1][:], w2_hi[:, w], w2_lo[:, w], x_hi[:, par, :],
                      x_lo[:, par, :]).then_inc(f_a, 1)

            def layer_h(t, c, w_hi, w_lo, in_hi, in_lo, s_in, s_free, s_done):
                s_free(t, c)
                w = slice(c * P, (c + 1) * P)
                for kc in range(FC):
                    if c == 0:
                        wait(pe, s_in, FC * t + kc + 1)
                    last = layer(bank_pv[c % 2][:], w_hi[:, kc, w], w_lo[:, kc, w], in_hi[kc], in_lo[kc],
                                 start=(kc == 0), stop=(kc == FC - 1))
                last.then_inc(s_done, 1)

            def layer_b(t, c):
                def free(t, c):
                    wait(pe, f_cg, FC * t - 1 + c) if c < 2 else wait(pe, f_bg, FC * t + c - 1)
                layer_h(t, c, h1_hi, h1_lo, a_hi, a_lo, f_al, free, f_b)

            def layer_c(t, c):
                def free(t, c):
                    wait(pe, f_bg, FC * (t + 1) - 1 + c) if c < 2 else wait(pe, f_cg, FC * t + c - 1)
                layer_h(t, c, h2_hi, h2_lo, b_hi, b_lo, f_bl, free, f_c)

            def layer_d(t, par):
                wait(pe, f_y, t)
                mm(bank_d[:], center[:], x_hi[:, par, :], start=True, stop=False)
                mm(bank_d[:], center[:], x_lo[:, par, :], start=False, stop=False)
                for kc in range(FC):
                    wait(pe, f_cl, FC * t + kc + 1)
                    last = three(bank_d[:], w3_hi[:, kc, :], w3_lo[:, kc, :], c_hi[kc], c_lo[kc],
                                 start=False, stop=(kc == FC - 1))
                last.then_inc(f_d, 1)

            def f_variance(t):
                wait(pe, f_sq, t + 1)
                wait(pe, f_r, t)
                if isinstance(t, int) and t == 0:
                    pe.wait_ge(s_lnv, NB)
                for j in range(NI):
                    last = mm(bank_v[:, j:j + 1], sq[:, j * P:(j + 1) * P], mean_of[:, 0:1], start=True, stop=True)
                last.then_inc(f_var, 1)

            def f_spread(t):
                wait(pe, f_i, t + 1)
                mm(bank_v[:], mean_exact[:], diag_hi[:], start=True, stop=False)
                mm(bank_v[:], mean_exact[:], diag_lo[:], start=False, stop=True).then_inc(f_w, 1)

            def tile(t, par, before, left):
                layer_b(t, 0)
                if two_before(t):
                    f_spread(t - 2)
                layer_b(t, 1)
                layer_b(t, 2)
                if before:
                    layer_d(t - 1, 1 - par)
                layer_b(t, 3)
                if before:
                    f_variance(t - 1)
                for what, c in mlp_order(left):
                    layer_a(t + 1, 1 - par, c) if what == "a" else layer_c(t, c)

            def mlp():
                layer_a(0, 0, 0)
                layer_a(0, 0, 1)
                out_proj(NB - 1, (NB - 1) % 2)
                layer_a(0, 0, 2)
                layer_a(0, 0, 3)
                var(NB - 1)
                batches(pe, tile)
                f_spread(NB - 2)
                layer_d(NB - 1, (NB - 1) % 2)
                f_variance(NB - 1)
                f_spread(NB - 1)

            with pe.If(some_low > 0):
                mlp()
            with pe.Else():
                exact_weights[0] = True
                mlp()

        @block.scalar
        def _(act):
            A = nc.scalar.activation
            nc.scalar.preload_act_table_set("natural_log_exp_and_others")
            act.wait_ge(s_prep_pe, 1)
            A(mq_f[:], bank_a[:, 0:H * L], ACT.Copy, scale=SCALE).then_inc(s_ln, 1)

            def q_evac(n, g):
                wait(act, s_q, G * n + g + 1)
                wait(act, s_qdma[g], 16 * 3 * R * n)
                A(q_hi[:, g, :], bank_a[:], ACT.Copy).then_inc(s_q_hi, 1)

            def k_evac(n, par, g):
                wait(act, s_k, G * n + g + 1)
                wait(act, s_st, NK * (n - 2) + NKG * (g + 1))
                A(ks[0:K3, par, g, :], bank_a[0:K3, :], ACT.Copy).then_inc(s_k_hi, 1)

            for g in range(G):
                q_evac(0, g)
                k_evac(0, 0, g)
            q_evac(1, 0)
            k_evac(1, 1, 0)
            act.wait_ge(s_const, 7)

            def exponentials(b, k):
                wait(act, s_st, NK * b + k + 1)
                wait(act, s_pv, NK * b + k - 3)
                A(probs[:, k % 4, :], bank_s[k % 2][:], ACT.Exp).then_inc(s_exp, 1)

            exponentials(0, 0)
            exponentials(0, 1)

            def batch(b, par, before, left):
                for what, k in steps(before, left):
                    if what == "o":
                        first_norm_a(b - 1)
                    elif what == "xr":
                        wait(act, s_x_again, 16 * (b + 1))
                        wait(act, s_o, b)
                        A(x_hi[:, 1, :], x_f[:, 1, :], ACT.Copy).then_inc(s_again_hi, 1)
                    elif what == "st":
                        exponentials(b, k)
                    elif what == "den":
                        denominator(b, k)
                    elif what == "q":
                        q_evac(b + k // G, k % G)
                    elif what == "k":
                        k_evac(b + k // G, par if k // G == 2 else 1 - par, k % G)
                    elif what == "rstd":
                        first_norm_b(b - 1)

            def denominator(b, u):
                n = u % 2
                ended = 0 if u < 0 else items.index(units[u] + (units[u][1],)) + 1
                wait(act, s_pv, NK * b + ended)
                wait(act, s_y, NU * b + u - 1)
                A(rden[:, n, :], bank_of(u % NU)[L:2 * L, :], ACT.Ln).then_inc(s_ln, 1)
                wait(act, s_ln, NU * b + u + 2)
                A(rden[:, n, :], rden[:, n, :], ACT.Exp, scale=-1.0).then_inc(s_rden, 1)

            def first_norm_a(n):
                wait(act, s_o, n + 1)
                wait(act, s_x1, n)
                A(sq_hi[:], bank_b[:], ACT.Square).then_inc(s_sq, 1)
                A(sq[:], bank_b[:], ACT.Square).then_inc(s_sq, 1)
                A(rc[:], bank_b[:], ACT.Copy).then_inc(s_rc, 1)

            def first_norm_b(n):
                wait(act, s_var, n + 1)
                A(rstd[:], bank_b[:], ACT.Ln, bias=eps_col[:, 0:1]).then_inc(s_lnv, 1)
                wait(act, s_lnv, n + 1)
                A(rstd[:], rstd[:], ACT.Exp, scale=-0.5).then_inc(s_rstd, 1)

            batches(act, batch)
            denominator(NB, -1)

            def a_chunk(t, c):
                n = FC * t + c + 1
                wait(act, f_a, 2 * n)
                wait(act, f_u, n - 2)
                A(t_act[c % 2], (bank_max, bank_s)[c % 2][0][:], ACT.Tanh, scale=s1h[:, c:c + 1]).then_inc(f_t, 1)

            def a_round(t, c):
                n = FC * t + c + 1
                wait(act, f_z, n)
                wait(act, f_b, FC * t)
                A(a_hi[c], u_act[c], ACT.Copy).then_inc(f_ah, 1)

            def gelu(t, c, s_in, scale, hi, s_next, s_used, used, s_done):
                wait(act, s_in, FC * t + c + 1)
                wait(act, s_used, used)
                A(g_act[c % 2], bank_pv[c % 2][:], ACT.Gelu, scale=scale[:, c:c + 1])
                wait(act, s_next[0], s_next[1])
                A(hi[c], bank_pv[c % 2][:], ACT.Gelu, scale=scale[:, c:c + 1]).then_inc(s_done, 1)

            def b_chunk(t, c):
                s_used, used = (f_cl, FC * (t - 1) + c + 3) if c < 2 else (f_bl, FC * t + c - 1)
                gelu(t, c, f_b, sh1, b_hi, (f_c, FC * t), s_used, used, f_bg)

            def c_chunk(t, c):
                s_used, used = (f_bl, FC * t + c + 3) if c < 2 else (f_cl, FC * t + c - 1)
                gelu(t, c, f_c, sh2, c_hi, (f_d, t), s_used, used, f_cg)

            def square(t):
                wait(act, f_d, t + 1)
                wait(act, f_var, t)
                A(sq[:], bank_a[:], ACT.Square).then_inc(f_sq, 1)

            def rstd_evac(t):
                wait(act, f_w, t + 1)
                A(rstd[:], bank_b[:], ACT.Copy).then_inc(f_r, 1)

            nc.scalar.preload_act_table_set("gelu_and_others")
            act.wait_ge(s_prep, PREP_ALL)
            a_chunk(0, 0)
            a_chunk(0, 1)
            first_norm_a(NB - 1)
            a_round(0, 0)
            for c in range(2, FC):
                a_chunk(0, c)
                a_round(0, c - 1)
            a_round(0, FC - 1)

            def act_step(t, layer, c, left):
                if layer == "a":
                    a_chunk(t + 1, c)
                    if c:
                        a_round(t + 1, c - 1)
                else:
                    c_chunk(t, c)
                    if left and c == FC - 2:
                        a_round(t + 1, FC - 1)

            def tile(t, par, before, left):
                b_chunk(t, 0)
                if two_before(t):
                    rstd_evac(t - 2)
                b_chunk(t, 1)
                b_chunk(t, 2)
                if before:
                    square(t - 1)
                b_chunk(t, 3)
                if isinstance(t, int) and t == 0:
                    nc.scalar.preload_act_table_set("natural_log_exp_and_others")
                    first_norm_b(NB - 1)
                    nc.scalar.preload_act_table_set("gelu_and_others")
                for layer, c in mlp_order(left):
                    act_step(t, layer, c, left)

            batches(act, tile)
            rstd_evac(NB - 2)
            square(NB - 1)
            rstd_evac(NB - 1)

        @block.vector
        def _(dve):
            V = nc.vector
            count = [0]

            def prep(ins):
                count[0] += 1
                ins.then_inc(s_prep, 1)
                dve.wait_ge(s_prep, count[0])

            def split_weight(hi, lo, raw):
                prep(V.tensor_copy(hi, raw))
                prep(V.tensor_tensor(lo, raw, hi.bitcast(F32), ALU.subtract))

            def round_x(n):
                wait(dve, s_x, 16 * (n + 1))
                wait(dve, s_k, G * n)
                V.tensor_copy(x_hi[:, 0, :], x_f[:, 0, :]).then_inc(s_x_hi, 1)

            def split_x(n):
                round_x(n)
                wait(dve, s_x_hi, n + 1)
                V.tensor_tensor(x_lo[:, 0, :], x_f[:, 0, :], x_hi[:, 0, :].bitcast(F32),
                                ALU.subtract).then_inc(s_x_lo, 1)

            prep(V.memset(eps_col[:], EPS))
            split_x(0)
            dve.wait_ge(s_load["attn"], 16 * (3 + R))
            for g in range(G):
                raw = wk_f[:, g * L:(g + 1) * L]
                for a in range(3):
                    split_weight(wk_hi[:, g, a, :], wk_lo[:, g, a, :], raw)
            dve.wait_ge(s_ln, 1)
            split_weight(mq_hi[:], mq_lo[:], mq_f[:])
            assert count[0] == PREP_MQ
            def v_evac(n, par):
                wait(dve, s_v, n + 1)
                wait(dve, s_pv, NK * (n - 1))
                V.tensor_copy(vs[:, par, :, :, 0:L].rearrange("p i g l -> p (i g) l"),
                              bank_a[:, 0:NI * G * L].rearrange("p (a l) -> p a l", l=L)).then_inc(s_v_out, 1)

            def q_evac(n, g):
                wait(dve, s_q_hi, G * n + g + 1)
                V.tensor_tensor(q_lo[:, g, :], bank_a[:], q_hi[:, g, :].bitcast(F32), ALU.subtract).then_inc(s_q_lo, 1)

            def k_evac(n, par, g):
                wait(dve, s_k_hi, G * n + g + 1)
                row = ks[L:2 * L, par, g, :]
                V.tensor_tensor(row, bank_a[L:2 * L, :], row.bitcast(F32),
                                ALU.subtract).then_inc(s_k_lo, 1)

            def max_unit(n, x):
                wait(dve, s_sx, NX * n + x + 1)
                V.memset(gate[:, x:x + 1], 0.0)
                for m, (g, i, h) in enumerate(max_units[x]):
                    width = (i + 1) * P
                    scores = bank_max[x % 2][:, m * 256:m * 256 + width]
                    at = (g * R + h) * NI + i
                    last = V.tensor_tensor_reduce(scores, scores, max_mask[:, T - width:T], 1.0, LOWEST, ALU.add,
                                                  ALU.max, mx[:, at:at + 1])
                last.then_inc(s_mx, 1)

            def minus_max(n, g):
                steps_before = NM_STEPS * (G * n + g)
                own = mx[:, g * NI * R:(g + 1) * NI * R]
                wait(dve, s_mx, NX * n + XG * (g + 1))
                V.tensor_scalar(nm[:, 0, :], own, -1.0, None, ALU.mult).then_inc(s_nm, 1)
                wait(dve, s_nm, steps_before + 1)
                V.scalar_tensor_tensor(nm[:, 1, :], own, -1.0, nm[:, 0, :].bitcast(F32), ALU.mult,
                                       ALU.subtract).then_inc(s_nm, 1)
                wait(dve, s_nm, steps_before + 2)
                wait(dve, s_mdma[1 - g], 32 * (n + g))
                for q in range(P // 32):
                    V.transpose(nmT[:, q * 32:(q + 1) * 32].bitcast(F32),
                                nm[q * 32:(q + 1) * 32, :, :].rearrange("p a r -> p (a r)").bitcast(F32)
                                ).then_inc(s_nm, 1)

            v_evac(0, 0)
            for g in range(G):
                q_evac(0, g)
                k_evac(0, 0, g)
            split_x(1)
            dve.wait_ge(s_prep_pe, 2)
            for h in range(H):
                bank = (bank_max + bank_s)[h // 2]
                rows = slice((h % R) * L, (h % R + 1) * L)
                step = V.tensor_copy(wvo[rows, h // R, :], bank[rows, (h % 2) * P:(h % 2 + 1) * P])
                count[0] += 1
                step.then_inc(s_prep, 1)
            dve.wait_ge(s_prep, count[0])
            prep(V.tensor_reduce(wvo_mean[:], wvo[:], AX_X, ALU.add))
            prep(V.tensor_scalar(wvo_mean[:], wvo_mean[:], 1.0 / P, None, ALU.mult))
            for g in range(G):
                prep(V.tensor_scalar(wvo[:, g, :], wvo[:, g, :], wvo_mean[:, g:g + 1], None, ALU.subtract))
            dve.wait_ge(s_const, 7)
            prep(V.tensor_copy(center[:], center_f[:]))
            prep(V.tensor_copy(mean_exact[:], mean_of[:]))
            assert count[0] == PREP_WVO
            q_evac(1, 0)
            k_evac(1, 1, 0)
            for x in range(XG):
                max_unit(0, x)
            minus_max(0, 0)
            for x in range(XG, XG + XL):
                max_unit(0, x)
            w3 = raw_hi[:, 2 * F:3 * F].rearrange("p (c n) -> p c n", c=FC)

            def mlp_weights(b, k):
                if b == 0 and k == 2:
                    dve.wait_ge(s_load["w123"], 48)
                    dve.wait_ge(s_load["small"], 80)
                    split_weight(w1_hi[:], w1_lo[:], raw_hi[:, 0:F])
                if b == 0 and k == 4:
                    split_weight(w2_hi[:], w2_lo[:], raw_hi[:, F:2 * F])
                if b == 0 and k == 6:
                    for c in range(FC):
                        prep(V.tensor_tensor(w3[:, c, :], w3[:, c, :], s3_row[:], ALU.mult))
                if b == 0 and k == 7:
                    prep(V.tensor_reduce(w3_mean[:], w3, AX_X, ALU.add))
                    prep(V.tensor_scalar(w3_mean[:], w3_mean[:], 1.0 / P, None, ALU.mult))
                if b == 0 and k == 8:
                    for c in range(FC):
                        prep(V.tensor_scalar(w3[:, c, :], w3[:, c, :], w3_mean[:, c:c + 1], None, ALU.subtract))
                if b == 0 and k == 10:
                    split_weight(w3_hi[:].rearrange("p c n -> p (c n)"), w3_lo[:].rearrange("p c n -> p (c n)"),
                                 raw_hi[:, 2 * F:3 * F])
                    assert count[0] == PREP_RAW
                if b == 0 and k in (12, 14, 16, 18):
                    c = (k - 12) // 2
                    dve.wait_ge(s_load["h1"], 16)
                    split_weight(h1_hi[:, c, :], h1_lo[:, c, :], raw_lo[:, c * F:(c + 1) * F])
                if b == 1 and k in (13, 15, 17, 19):
                    c = (k - 13) // 2
                    dve.wait_ge(s_load["h2"], 16)
                    split_weight(h2_hi[:, c, :], h2_lo[:, c, :], raw_hi[:, c * F:(c + 1) * F])
                if b == 1 and k in (2, 3):
                    lo = (w1_lo, w2_lo)[k - 2]
                    prep(V.tensor_reduce(low_parts[:, k - 2:k - 1], lo[:].bitcast(F32), AX_X, ALU.max,
                                         apply_absolute_value=True))
                if b == 1 and k in (4, 6, 8, 10) or b == NB - 2 and k in (4, 8, 12, 16):
                    c = k // 4 - 1 if b > 1 else (k - 4) // 2
                    lo, at = (h2_lo, 2 + FC + c) if b > 1 else (h1_lo, 2 + c)
                    prep(V.tensor_reduce(low_parts[:, at:at + 1], lo[:, c, :].bitcast(F32), AX_X, ALU.max,
                                         apply_absolute_value=True))
                if b == NB - 2 and k == 18:
                    prep(V.tensor_reduce(has_low[:], low_parts[:], AX_X, ALU.max))
                    prep(V.tensor_scalar(has_low[:], has_low[:], 0.0, None, ALU.is_gt))
                    assert count[0] == PREP_WIDE
                if b == NB - 1 and k == 4:
                    prep(V.tensor_scalar(s1h[:], s1h[:], 0.5, None, ALU.mult))
                    prep(V.tensor_tensor(s12h[:], s1h[:], s2[:], ALU.mult))
                    dve.wait_ge(s_prep_pe, 3)
                    prep(V.tensor_scalar(inexact[:], bank_a[0:1, 0:1], 0.0, None, ALU.is_gt))
                    assert count[0] == PREP_ALL

            def batch(b, par, before, left):
                for what, k in steps(before, left):
                    if what == "pv" and isinstance(b, int):
                        mlp_weights(b, k)
                    elif what == "v":
                        v_evac(b + 1, 1 - par)
                    elif what == "x":
                        round_x(b + 2)
                    elif what == "q":
                        q_evac(b + k // G, k % G)
                    elif what == "k":
                        k_evac(b + k // G, par if k // G == 2 else 1 - par, k % G)
                    elif what == "norm":
                        first_norm(b - 1)
                    elif what == "mx":
                        max_unit(b, k) if k < NX else max_unit(b + 1, k - NX)
                    elif what == "nm":
                        minus_max(b, k) if k < G else minus_max(b + 1, 0)
                    elif what == "y":
                        normalise(b, k, par)

            def normalise(b, u, par):
                g, i = units[u]
                if u < 0:
                    par = 1 - par
                wait(dve, s_rden, NU * b + u + 1)
                wait(dve, s_o, b - 1)
                for h in range(R):
                    last = V.tensor_tensor(ys[h * L:(h + 1) * L, par, g, i * P:(i + 1) * P],
                                           bank_of(u % NU)[0:L, h * P:(h + 1) * P],
                                           rden[:, u % 2, h * P:(h + 1) * P], ALU.mult)
                last.then_inc(s_y, 1)

            def first_norm(n):
                wait(dve, s_rstd, n + 1)
                V.tensor_tensor(x1[:, bass.ds(value(n * T), T)], rc[:], rstd[:], ALU.mult).then_inc(s_x1, 1)

            batches(dve, batch)

            def split_x1(t, par):
                wait(dve, f_d, t - 1)
                if isinstance(t, int) and t == 0:
                    dve.wait_ge(s_x1, 1)
                    dve.wait_ge(s_k, G * NB)
                source = x1[:, bass.ds(value(t * T), T)]
                V.tensor_copy(x_hi[:, par, :], source).then_inc(f_x_hi, 1)
                wait(dve, f_x_hi, t + 1)
                V.tensor_tensor(x_lo[:, par, :], source, x_hi[:, par, :].bitcast(F32), ALU.subtract).then_inc(f_x_lo, 1)

            def a_chunk(t, c):
                z1, z2 = (bank_max, bank_s)[c % 2]
                n = FC * t + c + 1
                wait(dve, f_t, n)
                wait(dve, f_al, n - FC)
                V.scalar_tensor_tensor(u_act[c], t_act[c % 2], 1.0, z1[:], ALU.add, ALU.mult).then_inc(f_u, 1)
                wait(dve, f_u, n)
                V.scalar_tensor_tensor(u_act[c], z2[:], s12h[:, c:c + 1], u_act[c], ALU.mult,
                                       ALU.mult).then_inc(f_z, 1)

            def b_chunk(t, c):
                wait(dve, f_bg, FC * t + c + 1)
                V.tensor_tensor(b_lo[c], g_act[c % 2], b_hi[c].bitcast(F32), ALU.subtract).then_inc(f_bl, 1)

            def c_chunk(t, c):
                wait(dve, f_cg, FC * t + c + 1)
                V.tensor_tensor(c_lo[c], g_act[c % 2], c_hi[c].bitcast(F32), ALU.subtract).then_inc(f_cl, 1)

            def guess(t):
                wait(dve, f_var, t + 1)
                wait(dve, f_n, NEWTON_STEPS * t)
                V.tensor_scalar(var_eps[:], bank_b[:, 0:NI], EPS, None, ALU.add).then_inc(f_v, 1)
                wait(dve, f_v, 2 * t + 1)
                V.tensor_scalar(var_half[:], var_eps[:], -0.5, None, ALU.mult).then_inc(f_v, 1)
                bits = newton_y[:].bitcast(I32)
                V.tensor_scalar(bits, var_eps[:].bitcast(I32), 1, None, ALU.logical_shift_right).then_inc(f_g, 1)
                wait(dve, f_g, 2 * t + 1)
                wait(dve, f_v, 2 * t + 2)
                V.tensor_scalar(bits, bits, -1.0, float(RSQRT_MAGIC), ALU.mult, ALU.add).then_inc(f_g, 1)

            def on_diagonals(t):
                wait(dve, f_n, NEWTON_STEPS * (t + 1))
                V.tensor_copy(y_hi[:], newton_y[:]).then_inc(f_yh, 1)
                wait(dve, f_yh, 2 * t + 1)
                V.tensor_tensor(y_lo[:], newton_y[:], y_hi[:].bitcast(F32), ALU.subtract).then_inc(f_yh, 1)
                wait(dve, f_yh, 2 * t + 2)
                for diag, y in ((diag_hi, y_hi), (diag_lo, y_lo)):
                    for j in range(NI):
                        last = V.tensor_scalar(diag[:, j * P:(j + 1) * P], unit_128[:], y[:, j:j + 1].bitcast(F32),
                                               None, ALU.mult)
                last.then_inc(f_i, 1)

            def second_norm(t, par):
                wait(dve, f_r, t + 1)
                wait(dve, f_store[par], 8 * (t - par) + 16)
                V.tensor_tensor(y_out[par], bank_a[:], rstd[:], ALU.mult).then_inc(f_y, 1)

            for par in range(2):
                V.memset(gate[:, par:par + 1], 0.0).then_inc(f_store[par], 16)
            split_x1(0, 0)
            normalise(NB, -1, 0)
            for c in range(FC):
                a_chunk(0, c)

            def tile(t, par, before, left):
                b_chunk(t, 0)
                if two_before(t):
                    second_norm(t - 2, par)
                b_chunk(t, 1)
                b_chunk(t, 2)
                if left:
                    split_x1(t + 1, 1 - par)
                b_chunk(t, 3)
                if before:
                    guess(t - 1)
                elif isinstance(t, int):
                    first_norm(NB - 1)
                for what, c in mlp_order(left):
                    a_chunk(t + 1, c) if what == "a" else c_chunk(t, c)
                    if before and (what, c) == (("a", 3) if left else ("c", 1)):
                        on_diagonals(t - 1)

            batches(dve, tile)
            second_norm(NB - 2, NB % 2)
            guess(NB - 1)
            on_diagonals(NB - 1)
            second_norm(NB - 1, (NB - 1) % 2)


def kernel(**inputs):
    import numpy as np
    import concourse.bacc as bacc
    from concourse.bass_utils import run_bass_kernel_spmd

    a = {n: np.asarray(v) for n, v in inputs.items()}
    NB, T, D = a["L0_attn_x"].shape
    HD = a["L0_attn_wk_up"].shape[1]
    H = a["L0_attn_wq"].shape[1] // HD
    F = a["L0_ffn_w1_w"].shape[0]
    FC = F // P

    def columns(s):
        return s.reshape(FC, P).T

    def wide(w):
        return w.T.reshape(w.shape[1] // P, P, w.shape[0]).transpose(1, 0, 2)

    laid = {
        "xT": a["L0_attn_x"].transpose(0, 2, 1),
        "wqT": a["L0_attn_wq"].reshape(D, H, HD).transpose(2, 1, 0),
        "wk_down": a["L0_attn_wk_down"],
        "wv_down": a["L0_attn_wv_down"],
        "wk_upT": a["L0_attn_wk_up"].T,
        "wv_upT": a["L0_attn_wv_up"].T,
        "wo": a["L0_attn_wo"].reshape(H, HD, D).transpose(1, 0, 2),
        "w1T": a["L0_ffn_w1_w"].T,
        "w1_s": columns(a["L0_ffn_w1_s"]),
        "w2T": a["L0_ffn_w2_w"].T,
        "w2_s": columns(a["L0_ffn_w2_s"]),
        "h1T": wide(a["L0_ffn_h1_w"]),
        "h1_s": columns(a["L0_ffn_h1_s"]),
        "h2T": wide(a["L0_ffn_h2_w"]),
        "h2_s": columns(a["L0_ffn_h2_s"]),
        "w3T": wide(a["L0_ffn_w3_w"]),
        "w3_s": a["L0_ffn_w3_s"],
    }
    laid = {n: np.ascontiguousarray(v) for n, v in laid.items()}
    nc = bacc.Bacc("TRN2", target_bir_lowering=False, num_devices=1)
    args = {n: nc.dram_tensor(f"{n}_dram", v.shape, F32, kind="ExternalInput").ap() for n, v in laid.items()}
    args["out"] = nc.dram_tensor("out_dram", (NB, D, T), F32, kind="ExternalOutput").ap()
    build_layer(nc, **args)
    r = run_bass_kernel_spmd(nc, [{f"{n}_dram": v for n, v in laid.items()}], core_ids=[0])
    return np.ascontiguousarray(r.results[0]["out_dram"].transpose(0, 2, 1))
```
